# Optimizing a Trainium2 kernel written in Bass

```python
import numpy as np
import jax
import jax.numpy as jnp

def _softmax(x, axis=-1):
    return jax.nn.softmax(x, axis=axis)

def _gelu(x):
    return jax.nn.gelu(x, approximate=True)

def _silu(x):
    return jax.nn.silu(x)

def _sigmoid(x):
    return jax.nn.sigmoid(x)

def _layernorm(x, axis=-1, eps=1e-05):
    m = jnp.mean(x, axis=axis, keepdims=True)
    v = jnp.var(x, axis=axis, keepdims=True)
    return (x - m) / jnp.sqrt(v + eps)

def _scatter_add(tgt, idx, src, axis=0):
    return tgt.at[idx].add(src)

def _segment_sum(src, seg, n):
    return jax.ops.segment_sum(src, seg, n)
kernel_name = 'mk_lm_tower_d1_tok_ids1024_r4_b682ab'

def setup_inputs(seed: int=0):
    np.random.seed(seed)
    _w = jnp.asarray

    def _rec_inputs():
        import jax
        import jax.numpy as jnp
        _rk = jax.random.key(seed)
        x = jax.random.randint(jax.random.fold_in(_rk, 1), (4, 1024), 0, 12564, jnp.int32)
        return x
    x = _rec_inputs()

    def _L0_tok_setup():
        import jax, jax.numpy as jnp
        import numpy as np
        VOCAB = 50257
        N_EMBD = 256
        B, T = (4, 1024)
        key = jax.random.key(seed)
        k_idx, = jax.random.split(key, 1)
        idx = jax.random.randint(k_idx, (B, T), 0, VOCAB, dtype=jnp.int64)
        projection = jnp.zeros((VOCAB, N_EMBD), dtype=jnp.float32)
        projection = projection.at[:N_EMBD, :].set(jnp.eye(N_EMBD, dtype=jnp.float32))
        return {'idx': idx, 'projection': projection}
    _L0_tok_all = _L0_tok_setup()
    _L0_tok_in = {k: v for k, v in _L0_tok_all.items() if k in ('projection',)}
    del _L0_tok_all

    def _L0_attn_setup():
        import jax, jax.numpy as jnp
        import numpy as np
        ALPHA = 1.0
        N_HEADS = 16
        key = jax.random.key(seed)
        ks = jax.random.split(key, 3)
        B, N, D = (2, 512, 256)
        x = jax.random.normal(ks[0], (B, N, D), dtype=jnp.float32)
        W_qkv = jax.random.normal(ks[1], (D, 3 * D), dtype=jnp.float32) * D ** (-0.5)
        b_qkv = jnp.zeros((3 * D,), dtype=jnp.float32)
        W_proj = jax.random.normal(ks[2], (D, D), dtype=jnp.float32) * D ** (-0.5)
        b_proj = jnp.zeros((D,), dtype=jnp.float32)
        return {'x': x, 'W_qkv': W_qkv, 'b_qkv': b_qkv, 'W_proj': W_proj, 'b_proj': b_proj}
    _L0_attn_all = _L0_attn_setup()
    _L0_attn_in = {k: v for k, v in _L0_attn_all.items() if k in ('W_qkv', 'b_qkv', 'W_proj', 'b_proj')}
    del _L0_attn_all

    def _L0_ffn_setup():
        import jax, jax.numpy as jnp
        import numpy as np
        QB = 127.0
        EPS = 1e-05

        def _ste(x, q):
            return x + jax.lax.stop_gradient(q - x)

        def bitlinear(x, W, b):
            w_scale = jnp.clip(jnp.mean(jnp.abs(W)), EPS, None)
            Wq = _ste(W, jnp.clip(jnp.round(W / w_scale), -1.0, 1.0) * w_scale)
            x_scale = jnp.clip(jnp.max(jnp.abs(x), axis=-1, keepdims=True), EPS, None)
            xq = _ste(x, jnp.clip(jnp.round(x * (QB / x_scale)), -QB - 1.0, QB) * (x_scale / QB))
            return jnp.einsum('bnd,hd->bnh', xq, Wq) + b
        key = jax.random.key(seed)
        k0, k1, k2 = jax.random.split(key, 3)
        B, N, D = (8, 1024, 256)
        H = int(D * 4.0)
        x = jax.random.normal(k0, (B, N, D), dtype=jnp.float32)
        W1 = jax.random.normal(k1, (H, D), dtype=jnp.float32) * 0.02
        b1 = jnp.zeros((H,), dtype=jnp.float32)
        W2 = jax.random.normal(k2, (D, H), dtype=jnp.float32) * 0.02
        b2 = jnp.zeros((D,), dtype=jnp.float32)
        return {'x': x, 'W1': W1, 'b1': b1, 'W2': W2, 'b2': b2}
    _L0_ffn_all = _L0_ffn_setup()
    _L0_ffn_in = {k: v for k, v in _L0_ffn_all.items() if k in ('W1', 'b1', 'W2', 'b2')}
    del _L0_ffn_all
    return {'x': x, 'L0_tok_projection': _L0_tok_in['projection'], 'L0_attn_W_qkv': _L0_attn_in['W_qkv'], 'L0_attn_b_qkv': _L0_attn_in['b_qkv'], 'L0_attn_W_proj': _L0_attn_in['W_proj'], 'L0_attn_b_proj': _L0_attn_in['b_proj'], 'L0_ffn_W1': _L0_ffn_in['W1'], 'L0_ffn_b1': _L0_ffn_in['b1'], 'L0_ffn_W2': _L0_ffn_in['W2'], 'L0_ffn_b2': _L0_ffn_in['b2']}

def reference(x, L0_tok_projection, L0_attn_W_qkv, L0_attn_b_qkv, L0_attn_W_proj, L0_attn_b_proj, L0_ffn_W1, L0_ffn_b1, L0_ffn_W2, L0_ffn_b2):
    import jax
    import jax.numpy as jnp

    def _L0_tok_ref(idx, projection):
        import jax, jax.numpy as jnp
        import numpy as np
        VOCAB = 50257
        N_EMBD = 256
        B, T = (4, 1024)
        return jnp.take(projection, idx, axis=0)

    def _L0_attn_ref(x, W_qkv, b_qkv, W_proj, b_proj):
        import jax, jax.numpy as jnp
        import numpy as np
        ALPHA = 1.0
        N_HEADS = 16
        B, N, D = x.shape
        H = N_HEADS
        hd = D // H
        qkv = (x @ W_qkv + b_qkv).reshape(B, N, 3, H, hd).transpose(2, 0, 3, 1, 4)
        q, k, v = (qkv[0], qkv[1], qkv[2])
        q_row_2 = jnp.max(jnp.sum(jnp.abs(q), axis=-1), axis=-1) ** 2
        k_col_2 = jnp.max(jnp.sum(jnp.abs(k), axis=-2), axis=-1) ** 2
        fro_q = jnp.sqrt(jnp.sum(q * q, axis=(-2, -1)))
        inf_xt = jnp.max(jnp.sum(jnp.abs(x), axis=-2), axis=-1)
        denom = fro_q * inf_xt[:, None]
        qk = jnp.einsum('bhnd,bhmd->bhnm', q, k)
        sim = -ALPHA * (q_row_2[:, :, None, None] - 2.0 * qk + k_col_2[:, :, None, None]) / denom[:, :, None, None]
        attn = jax.nn.softmax(sim, axis=-1)
        weighted = jnp.einsum('bhnm,bhmd->bhnd', attn, v)
        weighted = weighted.transpose(0, 2, 1, 3).reshape(B, N, D)
        return weighted @ W_proj + b_proj

    def _L0_ffn_ref(x, W1, b1, W2, b2):
        import jax, jax.numpy as jnp
        import numpy as np
        QB = 127.0
        EPS = 1e-05

        def _ste(x, q):
            return x + jax.lax.stop_gradient(q - x)

        def bitlinear(x, W, b):
            w_scale = jnp.clip(jnp.mean(jnp.abs(W)), EPS, None)
            Wq = _ste(W, jnp.clip(jnp.round(W / w_scale), -1.0, 1.0) * w_scale)
            x_scale = jnp.clip(jnp.max(jnp.abs(x), axis=-1, keepdims=True), EPS, None)
            xq = _ste(x, jnp.clip(jnp.round(x * (QB / x_scale)), -QB - 1.0, QB) * (x_scale / QB))
            return jnp.einsum('bnd,hd->bnh', xq, Wq) + b
        h = bitlinear(x, W1, b1)
        h = jax.nn.gelu(h, approximate=False)
        return bitlinear(h, W2, b2)
    h = _L0_tok_ref(x, L0_tok_projection)
    h = h + _L0_attn_ref(_layernorm(h, axis=-1), L0_attn_W_qkv, L0_attn_b_qkv, L0_attn_W_proj, L0_attn_b_proj)
    h = h + _L0_ffn_ref(_layernorm(h, axis=-1), L0_ffn_W1, L0_ffn_b1, L0_ffn_W2, L0_ffn_b2)
    return h

_drawn_inputs = setup_inputs


def setup_inputs(seed=0):
    import zlib

    import numpy as np

    out = dict(_drawn_inputs(seed))
    spreads = {'L0_attn_b_qkv': (0.0, 0.1),
     'L0_attn_b_proj': (0.0, 0.1),
     'L0_ffn_b1': (0.0, 0.1),
     'L0_ffn_b2': (0.0, 0.1)}
    factors = {}
    for name, (base, spread) in spreads.items():
        noise = np.random.default_rng([zlib.crc32(name.encode()), seed]).standard_normal(out[name].shape)
        drawn = base * np.exp(spread * noise) if base else spread * noise
        out[name] = jnp.asarray(drawn.astype(out[name].dtype))
    for name, factor in factors.items():
        out[name] = (out[name] * factor).astype(out[name].dtype)
    return out
```

```python
import concourse.bass as bass
from concourse import mybir
from contextlib import ExitStack

F32 = mybir.dt.float32
BF16 = mybir.dt.bfloat16
I32 = mybir.dt.int32
ALU = mybir.AluOpType
ACT = mybir.ActivationFunctionType
AX = mybir.AxisListType

B, N, D = 4, 1024, 256
H, HD = 16, 16
HID = 4 * D
P = 128
NT = N // P
DT = D // P
HT = HID // P
HPT = P // HD
GH = 4
NG = H // GH
SLOTS = NG * NT
HALF = 512
TERMS = 6
GUARD = TERMS * HD
EPS = 1e-5
QB = 127.0
MAGIC = 1.5 * 2.0 ** 23

K_RUNS = [(0, 3), (3, 2), (5, 1)]
Q_PART = [0, 0, 0, 1, 1, 2]

SETUP_UNITS = 6
CONSTANTS = 16
FRO2, FRO, K_SUM, K_MAX, X_SUM, Q_SUM, DENOM, TWICE, CONST, SHIFT = range(10)

F_ITEMS = {s: [] for s in range(SLOTS)}
R_ITEMS = {s: [] for s in range(SLOTS)}
for t in range(NT):
    F_ITEMS[2 + t].append(("proj", t))
    first = 11 + t if t < 4 else 15 + t
    F_ITEMS[first].append(("xq", t))
    F_ITEMS[first + 1].append(("xqT", t))
    F_ITEMS[first + 2].append(("up", t))
    down = 18 + t if t < 4 else 22 + t
    F_ITEMS[down].append(("gq", t))
    F_ITEMS[down + 1].append(("gT", t))
    F_ITEMS[down + 2].append(("down", t))
for s in range(SLOTS):
    F_ITEMS[s].sort(key=lambda it: it[1])
F_ITEMS[0].append(("load", 0))
F_ITEMS[10].append(("rstd", 0))
F_ITEMS[17].append(("gelu", 0))
F_ITEMS[25].append(("gelu", 1))
F_ITEMS[31].append(("store", 0))
R_ITEMS[0] += [("norm", 0), ("xT", 0), ("xT", 1)]
R_ITEMS[1] += [("xT", 2), ("xT", 3), ("xsum", 0)]
for u in range(4):
    R_ITEMS[2 + 2 * u].append(("q", u))
    R_ITEMS[10 + u].append(("k", u))
    R_ITEMS[18 + u].append(("v", u))
R_ITEMS[15] += [("norms", 0)]
R_ITEMS[16] += [("qrow", 0), ("qrow", 1), ("stat", 0), ("stat", 1)]
R_ITEMS[19] += [("fold", 0)]
R_ITEMS[21] += [("split", ("k", 0))]
R_ITEMS[22] += [("split", ("q", 0))]
R_ITEMS[24] += [("split", ("k", 1))]
R_ITEMS[25] += [("split", ("q", 1))]

SPLITS = [("k", 0), ("q", 0), ("k", 1), ("q", 1)]

UNITS_OF = {"proj": 1, "xqT": 1, "up": 2, "gT": 1, "down": 1,
            "xT": 1, "q": 1, "k": 1, "v": 1, "qrow": 1, "stat": 1}


def plan(with_f, with_r):
    items, first, n = [], {}, 0
    for s in range(SLOTS):
        here = (R_ITEMS[s] if with_r else []) + (F_ITEMS[s] if with_f else [])
        for it in here:
            if it[0] in UNITS_OF:
                first[it] = n
                n += UNITS_OF[it[0]]
        items.append(here)
    return items, first, n


R_ONLY, F_ONLY, BOTH = plan(False, True), plan(True, False), plan(True, True)
U_R, U_F = R_ONLY[2], F_ONLY[2]
assert U_R % 2 == 0 and U_F % 2 == 0 and BOTH[2] == U_R + U_F
BASE_0 = SETUP_UNITS + U_R
BASE_1 = BASE_0 + U_R


def rounds(b):
    return b * (U_R + U_F) + (BASE_1 - U_R - U_F)


def starts(b, n):
    return isinstance(b, int) and b == n


def pass_wait(eng, sem):
    eng.sem_inc(sem, 1)


class Chain:

    def __init__(self, eng, sem, base):
        self.eng, self.sem, self.base, self.n = eng, sem, base, 0

    def inc(self, ins):
        ins.then_inc(self.sem, 1)
        self.n += 1

    def wait(self):
        self.eng.wait_ge(self.sem, self.base + self.n)


F_STEPS = 2 * NT - 1 + 1 + 6 * NT + 5 * NT
R_STEPS = 53


def block_kernel(nc, x, table, w_qkv, b_qkv, w_proj, b_proj, w1, b1, w2, b2, out):
    x_v = x.rearrange("b (p t) -> b p t", t=NT)
    out_v = out.rearrange("b (p t) d -> b p t d", t=NT)
    ctx = ExitStack()
    with ctx:
        def sb(name, shape, dt=F32):
            return ctx.enter_context(nc.sbuf_tensor(name, shape, dt))

        def sem(name):
            return ctx.enter_context(nc.semaphore(name))

        parts_dram = nc.dram_tensor("parts_dram", (2, H, 3, HD, N), BF16, kind="Internal").ap()

        ident = sb("ident", [P, P])
        ident_bf = sb("ident_bf", [P, P], BF16)
        ones = sb("ones", [P, P])
        head_mask = sb("head_mask", [P, 32])
        guard_mask = sb("guard_mask", [P, 3])
        half_c = sb("half_c", [P, 2 * H])
        wqkv = sb("wqkv", [P, DT, 3 * D])
        wp = sb("wp", [P, DT, D])
        w1T = sb("w1T", [P, DT, HID], BF16)
        w2T = sb("w2T", [P, HT, D], BF16)
        w_scale = sb("w_scale", [P, 2])
        w_abs = sb("w_abs", [P, 2])
        w_inv = sb("w_inv", [P, 2])
        bqk = sb("bqk", [P, 4])
        bv = sb("bv", [P, 2, D])
        bp = sb("bp", [P, D])
        b1_row = sb("b1_row", [P, HID])
        b2_row = sb("b2_row", [P, D])
        idx_n = sb("idx_n", [P, NT], I32)
        xn = sb("xn", [P, NT, D])
        bst = sb("bst", [P, NT, 6])
        mv = sb("mv", [P, NT, 2])
        sd = sb("sd", [P, NT])
        xT = sb("xT", [P, DT, N])
        qk = sb("qk", [P, 2, DT, N])
        work = sb("work", [P, 4 * N])
        rest = work[:, 0:N]
        diag = work[:, 0:N].rearrange("p (c n) -> p c n", c=8)
        absq = work[:, N:3 * N].rearrange("p (i n) -> p i n", i=DT)
        part = work[:, N:4 * N].bitcast(BF16).rearrange("p (r c n) -> p r c n", r=2, c=3)
        stat = sb("stat", [P, 8])
        pair = sb("pair", [P, 4])
        st = sb("st", [P, 10, H])
        gpart = sb("gpart", [P, 3, H], BF16)
        gsel = sb("gsel", [P, H], F32)
        gtmp = sb("gtmp", [P, H], F32)
        gw = sb("gw", [P, H], BF16)
        scol = sb("scol", [P, DT])
        smul = sb("smul", [P, DT, HPT])
        vn = sb("vn", [P, NT, D])
        qh = [sb(f"qh{i}", [P, GH, N], BF16) for i in range(2)]
        kh = [sb(f"kh{i}", [P, GH, N], BF16) for i in range(2)]
        vs = [sb(f"vs{i}", [P, NT, GH, 32]) for i in range(2)]
        probs = sb("probs", [P, 2, GH, N])
        o_sb = sb("o_sb", [P, N])
        o_div = sb("o_div", [P, N])
        attn = sb("attn", [P, DT, N])
        idx_f = sb("idx_f", [P, NT], I32)
        h2 = sb("h2", [P, NT, D])
        bst2 = sb("bst2", [P, NT, 6])
        mv2 = sb("mv2", [P, NT, 2])
        sd2 = sb("sd2", [P, NT])
        xf = sb("xf", [P, D])
        sx = sb("sx", [P, NT, 4])
        sg = sb("sg", [P, NT, 4])
        xq = sb("xq", [P, 2, D], BF16)
        xqT = sb("xqT", [P, 2, DT, P], BF16)
        hid = sb("hid", [P, 4, HID])
        gq = sb("gq", [P, 2, HID], BF16)
        gqT = sb("gqT", [P, 2, HT, P], BF16)

        w1_raw = probs[:, 0, 0:2, :].rearrange("p a n -> p (a n)")
        w2_raw = probs[:, 0, 2:4, :].rearrange("p a n -> p (a n)")
        w1_bf = probs[:, 1, 0, :].bitcast(BF16)
        w2_bf = probs[:, 1, 1, :].bitcast(BF16)

        s_ps = ctx.enter_context(nc.psum_tensor("s_ps", [P, 2, 2, HALF], F32))
        o_ps = ctx.enter_context(nc.psum_tensor("o_ps", [P, 2, HALF], F32))
        m_ps = ctx.enter_context(nc.psum_tensor("m_ps", [P, 2, HALF], F32))

        w_in = sem("w_in")
        ffw_in = sem("ffw_in")
        rows_in = sem("rows_in")
        const_step = sem("const_step")
        setup_step = sem("setup_step")
        unit_full = sem("unit_full")
        unit_free = sem("unit_free")
        idx_n_in = sem("idx_n_in")
        idx_f_in = sem("idx_f_in")
        xn_in = sem("xn_in")
        h2_in = sem("h2_in")
        r_step = sem("r_step")
        r_var = sem("r_var")
        r_sd = sem("r_sd")
        xn_ready = sem("xn_ready")
        absq_ready = sem("absq_ready")
        diag_ready = sem("diag_ready")
        fro_sq = sem("fro_sq")
        fro_ready = sem("fro_ready")
        fold_ready = sem("fold_ready")
        part_ready = sem("part_ready")
        part_out = [sem(f"part_out{i}") for i in range(2)]
        staged = [sem(f"staged{i}") for i in range(2)]
        guard_set = sem("guard_set")
        v_staged = sem("v_staged")
        s_full = sem("s_full")
        exp_done = sem("exp_done")
        pv_done = sem("pv_done")
        o_read = sem("o_read")
        o_inv = sem("o_inv")
        o_norm = sem("o_norm")
        a_step = sem("a_step")
        attn_in = sem("attn_in")
        h2_base = sem("h2_base")
        f_step = sem("f_step")
        f_var = sem("f_var")
        f_sd = sem("f_sd")
        xq_ready = sem("xq_ready")
        h2_b2 = sem("h2_b2")
        gelu_done = sem("gelu_done")
        gq_ready = sem("gq_ready")
        out_done = sem("out_done")
        passed_pool = sem("passed_pool")
        passed_dve = sem("passed_dve")

        block = ctx.enter_context(nc.Block())

        def run(eng, setup, items_of, slot, flush):
            setup()

            def one_round(b, kind, base, attention=True):
                items, first, _ = kind
                for s in range(SLOTS):
                    if attention:
                        slot(b, s)
                    for it in items[s]:
                        items_of(it, b, base, first)
                if attention:
                    flush(b)

            one_round(-1, R_ONLY, SETUP_UNITS, attention=False)
            one_round(0, R_ONLY, BASE_0)
            with eng.Fori(1, B - 1) as b:
                one_round(b, BOTH, rounds(b))
            one_round(B - 1, F_ONLY, rounds(B - 1))
            one_round(B, F_ONLY, rounds(B - 1) + U_F, attention=False)

        @block.tensor
        def _(pe):
            def unit(u):
                pe.wait_ge(unit_free, u - 1)

            def setup():
                pe.wait_ge(const_step, CONSTANTS)
                for w in range(2):
                    if w == 0:
                        pe.wait_ge(setup_step, 1)
                    else:
                        pe.wait_ge(setup_step, 2)
                    nc.tensor.matmul(m_ps[:, w, 0:1], ones[:], w_abs[:, w:w + 1],
                                     start=True, stop=True).then_inc(unit_full, 1)
                for w in range(2):
                    pe.wait_ge(setup_step, 6 if w == 0 else 9)
                    for c in range(2):
                        u = 2 + 2 * w + c
                        unit(u)
                        bank = m_ps[:, c, :].bitcast(BF16).rearrange("p (j n) -> p j n", n=P)
                        for j in range(8):
                            if w == 0:
                                src = w1_bf[:, j * D + c * P:j * D + (c + 1) * P]
                            else:
                                src = w2_bf[:, c * HID + j * P:c * HID + (j + 1) * P]
                            last = nc.tensor.transpose(bank[:, j, :], src, ident_bf[:])
                        last.then_inc(unit_full, 1)

            def items_of(it, b, base, first):
                name, arg = it
                if name not in UNITS_OF:
                    return
                local = first[it]
                u = base + local
                bank = m_ps[:, local % 2, :]
                beta = b + 1 if name in ("xT", "q", "k", "v", "qrow", "stat") else b - 1
                needs = {"q": ("xT", 3), "k": ("xT", 3), "v": ("xT", 3), "up": ("xqT", arg),
                         "down": ("gT", arg)}.get(name)
                pe.wait_ge(unit_free, base + max(local - 1, first[needs] + 1 if needs else 0))
                if name == "xT":
                    dh, tg = arg // 2, arg % 2
                    pe.wait_ge(xn_ready, beta + 1)
                    for q in range(4):
                        last = nc.tensor.transpose(bank[:, q * P:(q + 1) * P],
                                                   xn[:, tg * 4 + q, dh * P:(dh + 1) * P], ident[:])
                    last.then_inc(unit_full, 1)
                elif name in ("q", "k"):
                    i, j = arg // 2, arg % 2
                    col = (0 if name == "q" else D) + i * P
                    for dh in range(DT):
                        last = nc.tensor.matmul(bank, wqkv[:, dh, col:col + P],
                                                xT[:, dh, j * HALF:(j + 1) * HALF],
                                                start=(dh == 0), stop=(dh == DT - 1))
                    last.then_inc(unit_full, 1)
                elif name == "v":
                    for r in range(2):
                        t = 2 * arg + r
                        for dh in range(DT):
                            last = nc.tensor.matmul(bank[:, r * D:(r + 1) * D],
                                                    xT[:, dh, t * P:(t + 1) * P],
                                                    wqkv[:, dh, 2 * D:3 * D],
                                                    start=(dh == 0), stop=(dh == DT - 1))
                    last.then_inc(unit_full, 1)
                elif name == "qrow":
                    pe.wait_ge(absq_ready, beta + 1)
                    for j in range(2):
                        r = 32 * (2 * arg + j)
                        last = nc.tensor.matmul(bank[r:r + 32, :], head_mask[:],
                                                absq[:, arg, j * HALF:(j + 1) * HALF],
                                                start=True, stop=True)
                    last.then_inc(unit_full, 1)
                elif name == "stat":
                    pe.wait_ge(diag_ready, 2 * beta + arg + 1)
                    nc.tensor.matmul(bank, ones[:],
                                     diag[:, 4 * arg:4 * arg + 4, :].rearrange("p c n -> p (c n)"),
                                     start=True, stop=True).then_inc(unit_full, 1)
                elif name == "proj":
                    pe.wait_ge(attn_in, (beta + 1) * 16 * GH * NG)
                    for k in range(DT):
                        last = nc.tensor.matmul(bank[:, 0:D], attn[:, k, arg * P:(arg + 1) * P],
                                                wp[:, k, :], start=(k == 0), stop=(k == DT - 1))
                    last.then_inc(unit_full, 1)
                elif name == "xqT":
                    pe.wait_ge(xq_ready, beta * NT + arg + 1)
                    view = bank.bitcast(BF16)
                    for k in range(DT):
                        last = nc.tensor.transpose(view[:, k * P:(k + 1) * P],
                                                   xq[:, arg % 2, k * P:(k + 1) * P], ident_bf[:])
                    last.then_inc(unit_full, 1)
                elif name == "up":
                    for c in range(2):
                        if c:
                            pe.wait_ge(unit_free, u)
                        for k in range(DT):
                            last = nc.tensor.matmul(m_ps[:, (local + c) % 2, :], xqT[:, arg % 2, k, :],
                                                    w1T[:, k, c * HALF:(c + 1) * HALF],
                                                    start=(k == 0), stop=(k == DT - 1))
                        last.then_inc(unit_full, 1)
                elif name == "gT":
                    pe.wait_ge(gq_ready, beta * NT + arg + 1)
                    view = bank.bitcast(BF16)
                    for k in range(HT):
                        last = nc.tensor.transpose(view[:, k * P:(k + 1) * P],
                                                   gq[:, arg % 2, k * P:(k + 1) * P], ident_bf[:])
                    last.then_inc(unit_full, 1)
                elif name == "down":
                    for k in range(HT):
                        last = nc.tensor.matmul(bank[:, 0:D], gqT[:, arg % 2, k, :], w2T[:, k, :],
                                                start=(k == 0), stop=(k == HT - 1))
                    last.then_inc(unit_full, 1)

            def pv_half(b, s, half):
                g, j = s // NT, s % NT
                for hh in range(GH):
                    last = nc.tensor.matmul(o_ps[32 * hh:32 * hh + 32, half, :],
                                            vs[g % 2][:, j, hh, :],
                                            probs[:, s % 2, hh, half * HALF:(half + 1) * HALF],
                                            start=(j == 0), stop=(j == NT - 1))
                if half == 1:
                    last.then_inc(pv_done, 1)

            def pv_waits(b, s):
                g, j = s // NT, s % NT
                pe.wait_ge(exp_done, (b * SLOTS + s + 1) * GH)
                if j == 0:
                    pe.wait_ge(v_staged, b * NG + g + 1)
                    if g > 0 or not (starts(b, 0)):
                        pe.wait_ge(o_read, b * NG + g)

            def slot(b, s):
                g, j = s // NT, s % NT
                if j == 0:
                    pe.wait_ge(staged[g % 2], (b * 2 + g // 2 + 1) * 16 * 9)
                    pe.wait_ge(guard_set, b * NG + g + 1)
                for hh in range(GH):
                    n = GH * s + hh
                    if n >= 2 or not (starts(b, 0)):
                        pe.wait_ge(exp_done, b * SLOTS * GH + n - 1)
                    for half in range(2):
                        last = nc.tensor.matmul(s_ps[:, n % 2, half, :],
                                                kh[g % 2][:, hh, j * P:(j + 1) * P],
                                                qh[g % 2][:, hh, half * HALF:(half + 1) * HALF],
                                                start=True, stop=True)
                    last.then_inc(s_full, 1)
                    if s > 0 and hh in (1, 2):
                        if hh == 1:
                            pv_waits(b, s - 1)
                        pv_half(b, s - 1, hh - 1)

            def flush(b):
                pv_waits(b, SLOTS - 1)
                pv_half(b, SLOTS - 1, 0)
                pv_half(b, SLOTS - 1, 1)

            pe.wait_ge(w_in, 16 * 4)
            run(pe, setup, items_of, slot, flush)

        @block.scalar
        def _(act):
            def setup():
                act.dma_start(wqkv[:], w_qkv.rearrange("(k p) n -> p k n", p=P)).then_inc(w_in, 16)
                act.dma_start(wp[:], w_proj.rearrange("(k p) n -> p k n", p=P)).then_inc(w_in, 16)
                act.dma_start(bqk[:, 0:2], b_qkv[0:D].rearrange("(i p) -> p i", p=P),
                              allow_slow_non_contiguous=True).then_inc(w_in, 16)
                act.dma_start(bqk[:, 2:4], b_qkv[D:2 * D].rearrange("(i p) -> p i", p=P),
                              allow_slow_non_contiguous=True).then_inc(w_in, 16)
                act.wait_ge(unit_free, SETUP_UNITS)

            def items_of(it, b, base, first):
                name, arg = it
                if name == "norms":
                    beta = b + 1
                    act.wait_ge(unit_free, base + first[("k", 3)] + 1)
                    if not starts(beta, 0):
                        for ring in range(2):
                            act.wait_ge(part_out[ring], beta * 2 * 3 * 16)
                    nc.scalar.activation(absq[:].rearrange("p i n -> p (i n)"),
                                         qk[:, 0, :, :].rearrange("p i n -> p (i n)"), ACT.Abs)\
                        .then_inc(absq_ready, 1)
                elif name == "gelu":
                    for q in range(4):
                        t = 4 * arg + q
                        act.wait_ge(unit_free, base + first[("up", t)] + 2)
                        nc.scalar.activation(hid[:, q, :], hid[:, q, :], ACT.Gelu).then_inc(gelu_done, 1)

            def slot(b, s):
                for hh in range(GH):
                    n = GH * s + hh
                    act.wait_ge(s_full, b * SLOTS * GH + n + 1)
                    if hh == 0 and (s >= 2 or not (starts(b, 0))):
                        act.wait_ge(pv_done, b * SLOTS + s - 1)
                    nc.scalar.activation(probs[:, s % 2, hh, :],
                                         s_ps[:, n % 2, :, :].rearrange("p a n -> p (a n)"),
                                         ACT.Exp).then_inc(exp_done, 1)

            run(act, setup, items_of, slot, lambda b: None)

        @block.sync
        def _(sp):
            def setup():
                sp.dma_start(idx_n[:], x_v[0]).then_inc(idx_n_in, 16)
                sp.dma_start(w1_raw.rearrange("p (j d) -> p j d", d=D),
                             w1.rearrange("(j p) d -> p j d", p=P)).then_inc(ffw_in, 16)
                sp.dma_start(w2_raw.rearrange("p (c n) -> p c n", n=HID),
                             w2.rearrange("(c p) n -> p c n", p=P)).then_inc(ffw_in, 16)
                for r in range(2):
                    sp.dma_start(bv[:, r, :], b_qkv[2 * D:3 * D].partition_broadcast(P)).then_inc(rows_in, 16)
                sp.dma_start(bp[:], b_proj.partition_broadcast(P)).then_inc(rows_in, 16)
                sp.dma_start(b1_row[:], b1.partition_broadcast(P)).then_inc(rows_in, 16)
                sp.dma_start(b2_row[:], b2.partition_broadcast(P)).then_inc(rows_in, 16)

            def stage(b, g):
                later = g >= 2 or not (starts(b, 0))
                if later:
                    sp.wait_ge(s_full, (b * NG + g - 1) * NT * GH)
                if g == 0:
                    for ring in range(2):
                        sp.wait_ge(part_out[ring], (b + 1) * 2 * 3 * 16)
                hs = slice(g * GH, (g + 1) * GH)
                for t0, n in K_RUNS:
                    sp.dma_start(kh[g % 2][t0 * HD:(t0 + n) * HD, :, :],
                                 parts_dram[1, hs, 0:n, :, :].rearrange("h c d n -> (c d) h n"))\
                      .then_inc(staged[g % 2], 16)
                for t, c in enumerate(Q_PART):
                    sp.dma_start(qh[g % 2][t * HD:(t + 1) * HD, :, :],
                                 parts_dram[0, hs, c, :, :].rearrange("h d n -> d h n"))\
                      .then_inc(staged[g % 2], 16)

            def attn_rows(b, g):
                sp.wait_ge(o_norm, b * NG + g + 1)
                if g == 0 and not (starts(b, 0)):
                    sp.wait_ge(unit_full, last_proj(b))
                for hh in range(GH):
                    r = (g % 2) * GH * HD + hh * HD
                    sp.dma_start(attn[r:r + HD, g // 2, :], o_sb[32 * hh:32 * hh + HD, :])\
                      .then_inc(attn_in, 16)

            def last_proj(b):
                kind = F_ONLY if isinstance(b, int) else BOTH
                return rounds(b) + kind[1][("proj", NT - 1)] + 1

            def items_of(it, b, base, first):
                name, arg = it
                if name == "norm" and not (starts(b, -1)):
                    sp.wait_ge(xn_in, (b + 1) * 16 * NT)
                    sp.dma_start(idx_n[:], x_v[b + 1]).then_inc(idx_n_in, 16)
                elif name == "load":
                    if not (starts(b, 1)):
                        sp.wait_ge(h2_in, (b - 1) * 16 * NT)
                    sp.dma_start(idx_f[:], x_v[b - 1]).then_inc(idx_f_in, 16)
                elif name == "split":
                    which, i = arg
                    beta = b + 1
                    w = 0 if which == "q" else 1
                    n = SPLITS.index(arg)
                    sp.wait_ge(part_ready, beta * 4 + n + 1)
                    if n == 0 and not (starts(b, -1)):
                        for ring in range(2):
                            sp.wait_ge(staged[ring], beta * 2 * 16 * 9)
                    for c in range(3):
                        sp.dma_start(parts_dram[w, i * HPT:(i + 1) * HPT, c, :, :], part[:, n % 2, c, :])\
                          .then_inc(part_out[n % 2], 16)
                    if n == 3:
                        stage(beta, 0)
                elif name == "store":
                    beta = b - 1
                    sp.wait_ge(unit_free, base + first[("down", NT - 1)] + 1)
                    sp.dma_start(out_v[beta], h2[:]).then_inc(out_done, 16)

            def slot(b, s):
                if s == 0:
                    stage(b, 1)
                if s % NT == 0 and s > 0:
                    g = s // NT
                    if g + 1 < NG:
                        stage(b, g + 1)
                    attn_rows(b, g - 1)

            def flush(b):
                attn_rows(b, NG - 1)

            run(sp, setup, items_of, slot, flush)
            sp.wait_ge(out_done, 16 * B)

        @block.gpsimd
        def _(pool):
            def setup():
                step = Chain(pool, const_step, 0)
                step.inc(nc.gpsimd.memset(ones[:], 1.0))
                step.inc(nc.gpsimd.memset(ident[:], 0.0))
                step.inc(nc.gpsimd.memset(head_mask[:], 0.0))
                step.inc(nc.gpsimd.memset(guard_mask[:], 0.0))
                step.inc(nc.gpsimd.memset(half_c[:], 0.5))
                step.wait()
                step.inc(nc.gpsimd.affine_select(out=ident[:], in_=ident[:], compare_op=ALU.not_equal,
                                                 fill=1.0, base=0, pattern=[[-1, P]],
                                                 channel_multiplier=1))
                step.inc(nc.gpsimd.affine_select(out=guard_mask[:], in_=guard_mask[:],
                                                 compare_op=ALU.not_equal, fill=1.0, base=-GUARD,
                                                 pattern=[[-1, 3]], channel_multiplier=1))
                step.inc(nc.gpsimd.affine_select(out=head_mask[:, 0:HPT], in_=ones[:, 0:HPT],
                                                 compare_op=ALU.is_ge, fill=0.0, base=0,
                                                 pattern=[[-HD, HPT]], channel_multiplier=1))
                step.wait()
                step.inc(nc.gpsimd.affine_select(out=head_mask[:, 0:HPT], in_=head_mask[:, 0:HPT],
                                                 compare_op=ALU.is_ge, fill=0.0, base=HD - 1,
                                                 pattern=[[HD, HPT]], channel_multiplier=-1))
                step.inc(nc.gpsimd.tensor_copy(ident_bf[:], ident[:]))
                step.wait()
                step.inc(nc.gpsimd.memset(kh[0][GUARD:P, :, :], 1.0))
                step.inc(nc.gpsimd.memset(kh[1][GUARD:P, :, :], 1.0))
                step.wait()
                for i in range(2):
                    step.inc(nc.gpsimd.memset(vs[i][:], 0.0))
                step.wait()
                for i in range(2):
                    step.inc(nc.gpsimd.memset(vs[i][:, :, :, HD:HD + 1], 1.0))
                step.wait()

            def gather(dst, idx, sem_in):
                pass_wait(pool, passed_pool)
                for t in range(NT):
                    nc.gpsimd.indirect_dma_start(
                        out=dst[:, t, :], out_offset=None, in_=table,
                        in_offset=bass.IndirectOffsetOnAxis(ap=idx[:, t:t + 1], axis=0)).then_inc(sem_in, 16)

            def root(var, root_out, sem_var, sem_root, beta):
                pool.wait_ge(sem_var, beta + 1)
                pass_wait(pool, passed_pool)
                nc.gpsimd.tensor_scalar(root_out[:], var, EPS, None, ALU.add).then_inc(sem_root, 1)
                pool.wait_ge(sem_root, 2 * beta + 1)
                nc.gpsimd.tensor_tensor(root_out[:], root_out[:], half_c[:, 0:NT], ALU.pow).then_inc(sem_root, 1)

            def items_of(it, b, base, first):
                name, arg = it
                if name == "norm":
                    beta = b + 1
                    pool.wait_ge(idx_n_in, (beta + 1) * 16)
                    if not (starts(b, -1)):
                        pool.wait_ge(absq_ready, beta)
                    gather(xn, idx_n, xn_in)
                    root(mv[:, :, 1], sd, r_var, r_sd, beta)
                elif it == ("stat", 0):
                    beta = b + 1
                    pool.wait_ge(fro_sq, beta + 1)
                    nc.gpsimd.tensor_tensor(st[:, FRO, :], st[:, FRO2, :], half_c[:, 0:H], ALU.pow)\
                        .then_inc(fro_ready, 1)
                elif name == "split" and arg == SPLITS[3]:
                    pool.wait_ge(unit_free, base + first[("v", 3)] + 1)
                    stage(b + 1, 0)
                elif name == "load":
                    beta = b - 1
                    pool.wait_ge(idx_f_in, (beta + 1) * 16)
                    if not (starts(b, 1)):
                        pool.wait_ge(out_done, beta * 16)
                    gather(h2, idx_f, h2_in)
                    pool.wait_ge(h2_in, (beta + 1) * 16 * NT)
                    if starts(b, 1):
                        pool.wait_ge(rows_in, 16 * 5)
                    nc.gpsimd.tensor_tensor(h2[:], h2[:], bp[:].unsqueeze(1).to_broadcast([P, NT, D]),
                                            ALU.add).then_inc(h2_base, 1)
                elif name == "rstd":
                    root(mv2[:, :, 1], sd2, f_var, f_sd, b - 1)
                elif name == "xq":
                    pool.wait_ge(xq_ready, (b - 1) * NT + arg + 1)
                    nc.gpsimd.tensor_tensor(h2[:, arg, :], h2[:, arg, :], b2_row[:], ALU.add).then_inc(h2_b2, 1)

            def stage(b, g):
                later = g >= 2 or not starts(b, 0)
                if g == 0:
                    pool.wait_ge(fold_ready, b + 1)
                if later:
                    pool.wait_ge(s_full, (b * NG + g - 1) * NT * GH)
                pass_wait(pool, passed_pool)
                pool.drain()
                nc.gpsimd.tensor_copy(qh[g % 2][GUARD:P, :, :],
                                      gw[GUARD:P, g * GH:(g + 1) * GH].unsqueeze(2)
                                      .to_broadcast([P - GUARD, GH, N])).then_inc(guard_set, 1)
                pool.wait_ge(guard_set, b * NG + g + 1)
                if later:
                    pool.wait_ge(pv_done, (b * NG + g - 1) * NT)
                pass_wait(pool, passed_pool)
                nc.gpsimd.tensor_copy(vs[g % 2][:, :, :, 0:HD],
                                      vn[:, :, g * GH * HD:(g + 1) * GH * HD]
                                      .rearrange("p t (h d) -> p t h d", d=HD)).then_inc(v_staged, 1)

            def normalise(b, g):
                pool.wait_ge(o_inv, b * NG + g + 1)
                nc.gpsimd.tensor_tensor(o_sb[:], o_sb[:], o_div[:], ALU.mult).then_inc(o_norm, 1)

            def slot(b, s):
                if s == 0:
                    stage(b, 1)
                if s % NT == 0 and s > 0:
                    g = s // NT
                    if g + 1 < NG:
                        stage(b, g + 1)
                    normalise(b, g - 1)

            def flush(b):
                normalise(b, NG - 1)

            run(pool, setup, items_of, slot, flush)

        @block.vector
        def _(dve):
            V = nc.vector

            def setup():
                step = Chain(dve, setup_step, 0)
                dve.wait_ge(ffw_in, 32)
                raws, terns = (w1_raw, w2_raw), (w1_bf, w2_bf)
                for w in range(2):
                    step.inc(V.tensor_reduce(w_abs[:, w:w + 1], raws[w], AX.X, ALU.add,
                                             apply_absolute_value=True))
                for w in range(2):
                    dve.wait_ge(unit_full, w + 1)
                    V.tensor_scalar(w_scale[:, w:w + 1], m_ps[:, w, 0:1], 1.0 / (HID * D), EPS,
                                    ALU.mult, ALU.max).then_inc(unit_free, 1)
                dve.wait_ge(unit_free, 2)
                step.inc(V.reciprocal(w_inv[:], w_scale[:]))
                step.wait()
                for w in range(2):
                    step.inc(V.tensor_scalar(raws[w], raws[w], w_inv[:, w:w + 1], MAGIC, ALU.mult, ALU.add))
                    step.wait()
                    step.inc(V.tensor_scalar(raws[w], raws[w], -MAGIC, 1.0, ALU.add, ALU.min))
                    step.wait()
                    step.inc(V.tensor_scalar(terns[w], raws[w], -1.0, None, ALU.max))
                for w in range(2):
                    for c in range(2):
                        dve.wait_ge(unit_full, 2 + 2 * w + c + 1)
                        bank = m_ps[:, c, :].bitcast(BF16)
                        if w == 0:
                            V.tensor_copy(w1T[:, c, :], bank).then_inc(unit_free, 1)
                        else:
                            V.tensor_copy(w2T[:, :, c * P:(c + 1) * P],
                                          bank.rearrange("p (j n) -> p j n", n=P)).then_inc(unit_free, 1)
                dve.wait_ge(w_in, 64)
                dve.wait_ge(rows_in, 16 * 5)
                dve.wait_ge(const_step, CONSTANTS)

            chains = {}

            def items_of(it, b, base, first):
                name, arg = it
                bank = None
                if name in UNITS_OF:
                    dve.wait_ge(unit_full, base + first[it] + 1)
                    bank = m_ps[:, first[it] % 2, :]
                if name == "norm":
                    chains["R"] = Chain(dve, r_step, (b + 1) * R_STEPS)
                elif name == "load":
                    chains["F"] = Chain(dve, f_step, (b - 1) * F_STEPS)
                if any(it in R_ITEMS[s] for s in range(SLOTS)):
                    prepare(it, b + 1, base, first, bank, chains["R"])
                else:
                    feed_forward(it, b - 1, base, first, bank, chains["F"])

            def prepare(it, beta, base, first, bank, step):
                name, arg = it
                if name == "norm":
                    dve.wait_ge(xn_in, (beta + 1) * 16 * NT)
                    for t in range(NT):
                        step.inc(V.bn_stats(bst[:, t, :], xn[:, t, :]))
                    step.wait()
                    pass_wait(dve, passed_dve)
                    for t in range(NT):
                        last = V.bn_aggr(mv[:, t, :], bst[:, t, :])
                    last.then_inc(r_var, 1)
                    dve.wait_ge(r_sd, 2 * (beta + 1))
                    step.inc(V.reciprocal(sd[:], sd[:]))
                    step.wait()
                    for t in range(NT):
                        last = V.tensor_scalar(xn[:, t, :], xn[:, t, :], mv[:, t, 0:1], sd[:, t:t + 1],
                                               ALU.subtract, ALU.mult)
                    last.then_inc(xn_ready, 1)
                elif name == "xT":
                    dh, tg = arg // 2, arg % 2
                    V.tensor_copy(xT[:, dh, tg * HALF:(tg + 1) * HALF], bank).then_inc(unit_free, 1)
                elif name == "xsum":
                    dve.wait_ge(unit_free, base + first[("xT", 3)] + 1)
                    for dh in range(DT):
                        step.inc(V.tensor_reduce(pair[:, dh:dh + 1], xT[:, dh, :], AX.X, ALU.add,
                                                 apply_absolute_value=True))
                    step.wait()
                    step.inc(V.tensor_tensor(stat[:, 6:7], pair[:, 0:1], pair[:, 1:2], ALU.max))
                elif name in ("q", "k"):
                    i, j = arg // 2, arg % 2
                    w = 0 if name == "q" else 1
                    V.tensor_scalar(qk[:, w, i, j * HALF:(j + 1) * HALF], bank,
                                    bqk[:, 2 * w + i:2 * w + i + 1], None, ALU.add).then_inc(unit_free, 1)
                elif name == "v":
                    if arg == 0 and not starts(beta, 0):
                        dve.wait_ge(v_staged, beta * NG)
                    V.tensor_tensor(vn[:, 2 * arg:2 * arg + 2, :],
                                    bank.rearrange("p (r d) -> p r d", r=2), bv[:], ALU.add)\
                        .then_inc(unit_free, 1)
                elif name == "norms":
                    dve.wait_ge(unit_free, base + first[("k", 3)] + 1)
                    for i in range(DT):
                        if i:
                            step.wait()
                        step.inc(V.tensor_tensor_reduce(out=rest, in0=qk[:, 0, i, :], in1=qk[:, 0, i, :],
                                                        scale=1.0, scalar=0.0, op0=ALU.mult, op1=ALU.add,
                                                        accum_out=stat[:, i:i + 1]))
                        step.inc(V.tensor_reduce(stat[:, 2 + i:3 + i], qk[:, 1, i, :], AX.X, ALU.add,
                                                 apply_absolute_value=True))
                        step.inc(V.tensor_reduce(stat[:, 4 + i:5 + i], qk[:, 1, i, :], AX.X, ALU.max,
                                                 apply_absolute_value=True))
                    step.wait()
                    for c in range(4):
                        last = V.tensor_scalar(diag[:, c, :], ident[:], stat[:, c:c + 1], None, ALU.mult)
                    last.then_inc(diag_ready, 1)
                elif name == "qrow":
                    r = 64 * arg
                    V.tensor_reduce(stat[r:r + 64, 7:8], bank[r:r + 64, :], AX.X, ALU.max)\
                        .then_inc(unit_free, 1)
                    if arg == 1:
                        dve.wait_ge(unit_free, base + first[it] + 1)
                        for c in range(4, 8):
                            last = V.tensor_scalar(diag[:, c, :], ident[:], stat[:, c:c + 1], None, ALU.mult)
                        last.then_inc(diag_ready, 1)
                elif name == "stat":
                    by_head = [bank[:, c * D:(c + 1) * D].rearrange("p (h d) -> p h d", d=HD) for c in range(2)]
                    if arg == 0:
                        V.tensor_reduce(st[:, FRO2, :], by_head[0], AX.X, ALU.add).then_inc(fro_sq, 1)
                        V.tensor_reduce(st[:, K_SUM, :], by_head[1], AX.X, ALU.max).then_inc(unit_free, 1)
                    else:
                        step.inc(V.tensor_reduce(st[:, K_MAX, :], by_head[0], AX.X, ALU.max))
                        step.inc(V.tensor_reduce(st[:, X_SUM, 0:1], bank[:, D:D + P], AX.X, ALU.max))
                        rows = bank[:, D + P:2 * D].rearrange("p (i j r) -> p i r j", i=DT, j=2)
                        V.tensor_reduce(st[:, Q_SUM, :].rearrange("p (i r) -> p i r", i=DT),
                                        rows[:, :, 0:HPT, :], AX.X, ALU.max).then_inc(unit_free, 1)
                elif name == "fold":
                    fold(beta, base, first, step)
                elif name == "split":
                    which, i = arg
                    n = SPLITS.index(arg)
                    src = qk[:, 0 if which == "q" else 1, i, :]
                    if n >= 2:
                        dve.wait_ge(part_out[n % 2], (beta * 2 + 1) * 3 * 16)
                    if which == "q":
                        step.inc(V.tensor_scalar(src, src, scol[:, i:i + 1], None, ALU.mult))
                        step.wait()
                    step.inc(V.tensor_copy(part[:, n % 2, 0, :], src))
                    step.wait()
                    step.inc(V.tensor_tensor(rest, src, part[:, n % 2, 0, :], ALU.subtract))
                    step.wait()
                    step.inc(V.tensor_copy(part[:, n % 2, 1, :], rest))
                    step.wait()
                    V.tensor_tensor(part[:, n % 2, 2, :], rest, part[:, n % 2, 1, :], ALU.subtract)\
                        .then_inc(part_ready, 1)
                    if n == 3:
                        assert step.n == R_STEPS, step.n

            def fold(beta, base, first, step):
                def op(ins):
                    step.inc(ins)
                    step.wait()

                dve.wait_ge(unit_free, base + first[("stat", 1)] + 1)
                dve.wait_ge(fro_ready, beta + 1)
                op(V.tensor_scalar(st[:, DENOM, :], st[:, FRO, :], st[:, X_SUM, 0:1], None, ALU.mult))
                op(V.reciprocal(st[:, DENOM, :], st[:, DENOM, :]))
                step.inc(V.tensor_scalar(st[:, TWICE, :], st[:, DENOM, :], 2.0, None, ALU.mult))
                step.inc(V.tensor_tensor(st[:, SHIFT, :], st[:, Q_SUM, :], st[:, K_MAX, :], ALU.mult))
                step.inc(V.tensor_tensor(st[:, K_SUM, :], st[:, K_SUM, :], st[:, K_SUM, :], ALU.mult))
                op(V.tensor_tensor(st[:, Q_SUM, :], st[:, Q_SUM, :], st[:, Q_SUM, :], ALU.mult))
                step.inc(V.tensor_tensor(st[:, SHIFT, :], st[:, SHIFT, :], st[:, TWICE, :], ALU.mult))
                op(V.tensor_tensor(st[:, CONST, :], st[:, Q_SUM, :], st[:, K_SUM, :], ALU.add))
                op(V.scalar_tensor_tensor(out=st[:, CONST, :], in0=st[:, CONST, :], scalar=-1.0,
                                          in1=st[:, DENOM, :], op0=ALU.mult, op1=ALU.mult))
                op(V.tensor_tensor(st[:, SHIFT, :], st[:, SHIFT, :], st[:, CONST, :], ALU.add))
                op(V.tensor_tensor(gtmp[:], st[:, CONST, :], st[:, SHIFT, :], ALU.subtract))
                op(V.tensor_copy(gpart[:, 0, :], gtmp[:]))
                op(V.tensor_tensor(gtmp[:], gtmp[:], gpart[:, 0, :], ALU.subtract))
                op(V.tensor_copy(gpart[:, 1, :], gtmp[:]))
                op(V.tensor_tensor(gpart[:, 2, :], gtmp[:], gpart[:, 1, :], ALU.subtract))
                op(V.tensor_scalar(gsel[:], gpart[:, 0, :], guard_mask[:, 0:1], None, ALU.mult))
                op(V.scalar_tensor_tensor(out=gsel[:], in0=gpart[:, 1, :], scalar=guard_mask[:, 1:2],
                                          in1=gsel[:], op0=ALU.mult, op1=ALU.add))
                op(V.tensor_tensor(smul[:], head_mask[:, 0:HPT].unsqueeze(1).to_broadcast([P, DT, HPT]),
                                   st[:, TWICE, :].rearrange("p (i h) -> p i h", i=DT), ALU.mult))
                op(V.tensor_reduce(scol[:], smul[:], AX.X, ALU.add))
                if not starts(beta, 0):
                    dve.wait_ge(guard_set, beta * NG)
                V.scalar_tensor_tensor(out=gw[:], in0=gpart[:, 2, :], scalar=guard_mask[:, 2:3],
                                       in1=gsel[:], op0=ALU.mult, op1=ALU.add).then_inc(fold_ready, 1)

            def quantise(step, src, scales, w, dst, ready):
                def op(ins):
                    step.inc(ins)
                    step.wait()

                op(V.tensor_reduce(scales[:, 0:1], src, AX.X, ALU.max, apply_absolute_value=True))
                op(V.tensor_scalar(scales[:, 1:2], scales[:, 0:1], EPS, 1.0 / QB, ALU.max, ALU.mult))
                op(V.reciprocal(scales[:, 2:3], scales[:, 1:2]))
                step.inc(V.tensor_scalar(scales[:, 3:4], scales[:, 1:2], w_scale[:, w:w + 1], None, ALU.mult))
                op(V.tensor_scalar(src, src, scales[:, 2:3], MAGIC, ALU.mult, ALU.add))
                V.tensor_scalar(dst, src, -MAGIC, QB, ALU.add, ALU.min).then_inc(ready, 1)

            def feed_forward(it, beta, base, first, bank, step):
                name, t = it
                if name == "proj":
                    if t == 0:
                        dve.wait_ge(h2_base, beta + 1)
                    V.tensor_tensor(h2[:, t, :], bank[:, 0:D], h2[:, t, :], ALU.add).then_inc(unit_free, 1)
                    dve.wait_ge(unit_free, base + first[it] + 1)
                    step.inc(V.bn_stats(bst2[:, t, :], h2[:, t, :]))
                    step.wait()
                    pass_wait(dve, passed_dve)
                    aggr = V.bn_aggr(mv2[:, t, :], bst2[:, t, :])
                    if t == NT - 1:
                        aggr.then_inc(f_var, 1)
                    else:
                        step.inc(aggr)
                elif name == "rstd":
                    dve.wait_ge(f_sd, 2 * (beta + 1))
                    step.inc(V.reciprocal(sd2[:], sd2[:]))
                elif name == "xq":
                    step.wait()
                    step.inc(V.tensor_scalar(xf[:], h2[:, t, :], mv2[:, t, 0:1], sd2[:, t:t + 1],
                                             ALU.subtract, ALU.mult))
                    step.wait()
                    quantise(step, xf[:], sx[:, t, :], 0, xq[:, t % 2, :], xq_ready)
                elif name == "xqT":
                    V.tensor_copy(xqT[:, t % 2, :, :].rearrange("p k n -> p (k n)"),
                                  bank.bitcast(BF16)[:, 0:D]).then_inc(unit_free, 1)
                elif name == "up":
                    step.wait()
                    for c in range(2):
                        u = base + first[it] + c
                        dve.wait_ge(unit_full, u + 1)
                        V.scalar_tensor_tensor(out=hid[:, t % 4, c * HALF:(c + 1) * HALF],
                                               in0=m_ps[:, (first[it] + c) % 2, :], scalar=sx[:, t, 3:4],
                                               in1=b1_row[:, c * HALF:(c + 1) * HALF],
                                               op0=ALU.mult, op1=ALU.add).then_inc(unit_free, 1)
                elif name == "gq":
                    dve.wait_ge(gelu_done, beta * NT + t + 1)
                    quantise(step, hid[:, t % 4, :], sg[:, t, :], 1, gq[:, t % 2, :], gq_ready)
                elif name == "gT":
                    V.tensor_copy(gqT[:, t % 2, :, :].rearrange("p k n -> p (k n)"),
                                  bank.bitcast(BF16)).then_inc(unit_free, 1)
                elif name == "down":
                    step.wait()
                    dve.wait_ge(h2_b2, beta * NT + t + 1)
                    V.scalar_tensor_tensor(out=h2[:, t, :], in0=bank[:, 0:D], scalar=sg[:, t, 3:4],
                                           in1=h2[:, t, :], op0=ALU.mult, op1=ALU.add)\
                        .then_inc(unit_free, 1)
                    if t == NT - 1:
                        assert step.n == F_STEPS, step.n

            def divide(b, g):
                dve.wait_ge(pv_done, b * SLOTS + (g + 1) * NT)
                if g > 0 or not starts(b, 0):
                    dve.wait_ge(attn_in, (b * NG + g) * 16 * GH)
                V.tensor_copy(o_sb[:], o_ps[:].rearrange("p a n -> p (a n)")).then_inc(o_read, 1)
                dve.wait_ge(o_read, b * NG + g + 1)
                pass_wait(dve, passed_dve)
                V.stream_shuffle(o_div[:], o_sb[:], [HD] * 32).then_inc(a_step, 1)
                dve.wait_ge(a_step, b * NG + g + 1)
                V.reciprocal(o_div[:], o_div[:]).then_inc(o_inv, 1)

            def slot(b, s):
                if s % NT == 0 and s > 0:
                    divide(b, s // NT - 1)

            run(dve, setup, items_of, slot, lambda b: divide(b, NG - 1))


_INS = ["x", "L0_tok_projection", "L0_attn_W_qkv", "L0_attn_b_qkv", "L0_attn_W_proj",
        "L0_attn_b_proj", "L0_ffn_W1", "L0_ffn_b1", "L0_ffn_W2", "L0_ffn_b2"]


def kernel(**inputs):
    import numpy as np
    import concourse.bacc as bacc
    from concourse.bass_utils import run_bass_kernel_spmd

    nc = bacc.Bacc("TRN2", target_bir_lowering=False, num_devices=1)
    arrays, args = {}, []
    for name in _INS:
        a = np.ascontiguousarray(inputs[name])
        arrays[f"in_{name}"] = a
        args.append(nc.dram_tensor(f"in_{name}", a.shape, mybir.dt.from_np(a.dtype), kind="ExternalInput").ap())
    out = nc.dram_tensor("out_h", (B, N, D), F32, kind="ExternalOutput").ap()
    block_kernel(nc, *args, out)
    r = run_bass_kernel_spmd(nc, [arrays], core_ids=[0])
    return r.results[0]["out_h"]
```

```python
import concourse.bass as bass
from concourse import mybir
from contextlib import ExitStack

F32 = mybir.dt.float32
BF16 = mybir.dt.bfloat16
I32 = mybir.dt.int32
ALU = mybir.AluOpType
ACT = mybir.ActivationFunctionType
AX = mybir.AxisListType

B, N, D = 4, 1024, 256
H, HD = 16, 16
HID = 4 * D
P = 128
NT = N // P
DT = D // P
HT = HID // P
HPT = P // HD
GH = 4
NG = H // GH
SLOTS = NG * NT
HALF = 512
TERMS = 6
GUARD = TERMS * HD
EPS = 1e-5
LIMIT = 20.0
QB = 127.0
MAGIC = 1.5 * 2.0 ** 23

K_RUNS = [(0, 3), (3, 2), (5, 1)]
Q_PART = [0, 0, 0, 1, 1, 2]

FILLS = 8
CONSTANTS = 10
FRO2, FRO, K_SUM, K_MAX, X_SUM, Q_SUM, DENOM, TWICE, CONST, SHIFT = range(10)


def table(*rows):
    items = {s: [] for s in range(SLOTS)}
    for name, arg, s in rows:
        items[s].append((name, arg))
    return items


def preparation(gather, stats, norm, xT, q, k, v, xsum, sq, sk, diag, qrow, stat, fold, split, stage):
    return table(("stats", 0, stats), ("norm", 0, norm),
                 *[("xT", u, xT[u]) for u in range(4)],
                 ("gather", 0, gather), *[("q", u, q[u]) for u in range(4)],
                 *[("k", u, k[u]) for u in range(4)],
                 ("xsum", 0, xsum), *[("sq", i, sq[i]) for i in range(DT)],
                 *[("sk", i, sk[i]) for i in range(DT)], ("diag", 0, diag),
                 ("qrow", 0, qrow), ("qrow", 1, qrow), ("stat", 0, stat[0]), ("stat", 1, stat[1]),
                 ("fold", 0, fold),
                 *[("split", which, split[n]) for n, which in enumerate(SPLITS)], ("stage", 0, stage),
                 *[("v", u, v[u]) for u in range(4)])


def feed_forwards(load, base, proj, rstd, xq, xqT, up, gelu, gq, gT, down, store):
    rows = [("load", 0, load), ("base", 0, base), ("rstd", 0, rstd)]
    for t in range(NT):
        rows += [("down", t, down[t]), ("gT", t, gT[t]), ("gq", t, gq[t]), ("up", t, up[t]),
                 ("xqT", t, xqT[t]), ("xq", t, xq[t]), ("proj", t, proj[t])]
    rows.sort(key=lambda row: row[2])
    for tiles, s in gelu:
        rows.append(("gelu", tiles, s))
    return table(*rows, ("store", 0, store))

SPLITS = [("k", 0), ("q", 0), ("k", 1), ("q", 1)]

W_ITEMS = table(("wload", 0, 1), ("wabs", 0, 21), ("wsum", 0, 22), ("wsum", 1, 22),
                ("tern", 0, 23), ("tern", 1, 25), ("wT", 0, 25), ("wT", 1, 25), ("wT", 2, 28), ("wT", 3, 28))
W_NAMES = ("wload", "wabs", "wsum", "tern", "wT")

R_ITEMS = preparation(gather=8, stats=0, norm=1, xT=(2, 2, 2, 2), q=(4, 4, 5, 5), k=(5, 5, 6, 6),
                      v=(19, 19, 26, 26), xsum=3, sq=(4, 5), sk=(6, 7), diag=7, qrow=8, stat=(9, 9),
                      fold=10, split=(11, 13, 28, 31), stage=26)
F_ITEMS = feed_forwards(load=3, base=6, proj=(8, 8, 9, 9, 10, 10, 11, 11), rstd=12,
                        xq=(13, 13, 15, 16, 17, 19, 20, 22), xqT=(14, 15, 16, 17, 19, 21, 23, 24),
                        up=(15, 16, 17, 18, 20, 22, 24, 25),
                        gelu=((range(0, 4), 18), (range(4, 8), 25)),
                        gq=(19, 21, 22, 23, 26, 27, 28, 29), gT=(20, 22, 23, 24, 27, 28, 29, 30),
                        down=(21, 23, 24, 25, 28, 29, 30, 31), store=31)
R_FIRST = preparation(gather=6, stats=1, norm=1, xT=(1, 1, 1, 1), q=(2, 3, 4, 5), k=(6, 7, 8, 9),
                      v=(16, 18, 20, 22), xsum=2, sq=(4, 6), sk=(8, 10), diag=11, qrow=12,
                      stat=(12, 13), fold=14, split=(15, 16, 24, 26), stage=24)
F_LAST = feed_forwards(load=3, base=5, proj=(8, 8, 8, 8, 8, 8, 8, 8), rstd=9,
                       xq=(10, 11, 12, 13, 15, 16, 17, 18), xqT=(11, 12, 13, 14, 16, 17, 20, 21),
                       up=(12, 13, 14, 15, 17, 18, 22, 23), gelu=((range(0, 4), 15), (range(4, 8), 23)),
                       gq=(16, 16, 18, 19, 24, 24, 26, 26), gT=(17, 18, 19, 20, 25, 25, 27, 28),
                       down=(18, 19, 20, 21, 26, 27, 28, 29), store=29)
PRE_ITEMS = table(("stats", 0, 0), ("norm", 0, 0), *[("xT", u, 0) for u in range(4)], ("gather", 0, 0),
                  ("q", 0, 1), ("k", 0, 1), ("xsum", 0, 1), ("q", 1, 1), ("k", 1, 1), ("q", 2, 1), ("sq", 0, 1),
                  ("k", 2, 1), ("sk", 0, 1), ("q", 3, 1), ("k", 3, 1), ("sq", 1, 1),
                  ("sk", 1, 1), ("v", 0, 1), ("diag", 0, 1), ("v", 1, 1), ("qrow", 0, 2), ("qrow", 1, 2),
                  ("stat", 0, 2), ("stat", 1, 2), ("fold", 0, 2), ("v", 2, 2), ("v", 3, 2),
                  ("split", SPLITS[0], 3), ("split", SPLITS[1], 3), ("stage", 0, 3),
                  ("split", SPLITS[2], 4), ("split", SPLITS[3], 4))
TAIL_ITEMS = table(("base", 0, 0), *[("proj", t, 0) for t in range(NT)], ("rstd", 0, 0),
                   *[(name, range(t, t + 1) if name == "gelu" else t, n + 2)
                     for n in range(-1, NT + 2)
                     for name, t in (("xq", n + 1), ("turn", n - 2), ("up", n), ("gelu", n),
                                     ("xqT", n + 1), ("gq", n - 1), ("down", n - 2)) if 0 <= t < NT],
                   ("store", 0, SLOTS - 1))

UNITS_OF = {"proj": 1, "xqT": 1, "up": 2, "gT": 1, "down": 1,
            "wsum": 1, "wT": 1, "xT": 1, "q": 1, "k": 1, "v": 1, "qrow": 1, "stat": 1}


def plan(*tables):
    items, first, n = [], {}, 0
    for s in range(SLOTS):
        here = [it for table in tables for it in table[s]]
        for it in here:
            if it[0] in UNITS_OF:
                first[it] = n
                n += UNITS_OF[it[0]]
        items.append(here)
    return items, first, n


ALONE, FIRST = plan(PRE_ITEMS), plan(R_FIRST, W_ITEMS)
BOTH, LAST, TAIL = plan(R_ITEMS, F_ITEMS), plan(F_LAST), plan(TAIL_ITEMS)
assert all(kind[2] % 2 == 0 for kind in (ALONE, FIRST, BOTH, LAST))
BASE_0 = ALONE[2]
BASE_1 = BASE_0 + FIRST[2]


def rounds(b):
    return b * BOTH[2] + (BASE_1 - BOTH[2])


def units_before(kind, slot):
    return sum(UNITS_OF.get(it[0], 0) for s in range(slot) for it in kind[0][s])


def starts(b, n):
    return isinstance(b, int) and b == n


def pass_wait(eng, sem):
    eng.sem_inc(sem, 1)


class Chain:

    def __init__(self, eng, sem, base):
        self.eng, self.sem, self.base, self.n = eng, sem, base, 0

    def inc(self, ins):
        ins.then_inc(self.sem, 1)
        self.n += 1

    def wait(self):
        self.eng.wait_ge(self.sem, self.base + self.n)


F_STEPS = 2 * NT - 1 + 1 + 6 * NT + 5 * NT
R_STEPS = 51


def block_kernel(nc, x, table, w_qkv, b_qkv, w_proj, b_proj, w1, b1, w2, b2, out):
    x_v = x.rearrange("b (p t) -> b p t", t=NT)
    out_v = out.rearrange("b (p t) d -> b p t d", t=NT)
    ctx = ExitStack()
    with ctx:
        def sb(name, shape, dt=F32):
            return ctx.enter_context(nc.sbuf_tensor(name, shape, dt))

        def sem(name):
            return ctx.enter_context(nc.semaphore(name))

        parts_dram = nc.dram_tensor("parts_dram", (2, H, 3, HD, N), BF16, kind="Internal").ap()

        inv_dram = nc.dram_tensor("inv_dram", (GH, N), F32, kind="Internal").ap()

        ident = sb("ident", [P, P])
        ident_bf = sb("ident_bf", [P, P], BF16)
        ones = sb("ones", [P, P])
        head_mask = sb("head_mask", [P, 32])
        guard_mask = sb("guard_mask", [P, 3])
        half_c = sb("half_c", [P, 2 * H])
        wqkv = sb("wqkv", [P, DT, 3 * D])
        wp = sb("wp", [P, DT, D])
        w1T = sb("w1T", [P, DT, HID], BF16)
        w2T = sb("w2T", [P, HT, D], BF16)
        w_scale = sb("w_scale", [P, 2])
        w_abs = sb("w_abs", [P, 2])
        w_half = sb("w_half", [P, 4])
        bqk = sb("bqk", [P, 4])
        bv = sb("bv", [P, 2, D])
        bp = sb("bp", [P, D])
        b1_row = sb("b1_row", [P, HID])
        b2_row = sb("b2_row", [P, D])
        idx_n = sb("idx_n", [P, NT], I32)
        xn = sb("xn", [P, NT, D])
        bst = sb("bst", [P, NT, 6])
        mv = sb("mv", [P, NT, 2])
        sd = sb("sd", [P, NT])
        xT = sb("xT", [P, DT, N])
        qk = sb("qk", [P, 2, DT, N])
        work = sb("work", [P, 4 * N])
        rest = work[:, 0:N]
        diag = work[:, 0:N].rearrange("p (c n) -> p c n", c=8)
        absq = work[:, N:3 * N].rearrange("p (i n) -> p i n", i=DT)
        part = work[:, N:4 * N].bitcast(BF16).rearrange("p (r c n) -> p r c n", r=2, c=3)
        stat = sb("stat", [P, 8])
        pair = sb("pair", [P, 4])
        st = sb("st", [P, 10, H])
        gpart = sb("gpart", [P, 3, H], BF16)
        gsel = sb("gsel", [P, H], F32)
        gtmp = sb("gtmp", [P, H], F32)
        gw = sb("gw", [P, H])
        gw_last = sb("gw_last", [P, GH])
        scol = sb("scol", [P, DT])
        smul = sb("smul", [P, DT, HPT])
        bound = sb("bound", [P, 1])
        wide = sb("wide", [P, 1], I32)
        top = sb("top", [P, 2])
        top_parts = sb("top_parts", [P, P], BF16)
        vn = sb("vn", [P, NT, D])
        qh = [sb(f"qh{i}", [P, GH, N], BF16) for i in range(2)]
        kh = [sb(f"kh{i}", [P, GH, N], BF16) for i in range(2)]
        vs = [sb(f"vs{i}", [P, NT, GH, 32]) for i in range(2)]
        probs = sb("probs", [P, 2, GH, N])
        o_sb = sb("o_sb", [P, N])
        o_div = sb("o_div", [P, N])
        sums = sb("sums", [P, GH * N // P])
        attn = sb("attn", [P, DT, N])
        idx_f = sb("idx_f", [P, NT], I32)
        h2 = sb("h2", [P, NT, D])
        bst2 = sb("bst2", [P, NT, 6])
        mv2 = sb("mv2", [P, NT, 2])
        sd2 = sb("sd2", [P, NT])
        xf = sb("xf", [P, D])
        sx = sb("sx", [P, NT, 4])
        sg = sb("sg", [P, NT, 4])
        xq = sb("xq", [P, 2, D], BF16)
        xqT = sb("xqT", [P, 2, DT, P], BF16)
        hid = sb("hid", [P, 4, HID])
        gq = sb("gq", [P, 2, HID], BF16)
        gqT = sb("gqT", [P, 2, HT, P], BF16)

        w1_raw = hid[:, 0:2, :].rearrange("p a n -> p (a n)")
        w2_raw = hid[:, 2:4, :].rearrange("p a n -> p (a n)")
        w1_bf = h2[:, 0:4, :].rearrange("p a n -> p (a n)").bitcast(BF16)
        w2_bf = h2[:, 4:8, :].rearrange("p a n -> p (a n)").bitcast(BF16)

        s_ps = ctx.enter_context(nc.psum_tensor("s_ps", [P, 2, 2, HALF], F32))
        o_ps = ctx.enter_context(nc.psum_tensor("o_ps", [P, 2, HALF], F32))
        m_ps = ctx.enter_context(nc.psum_tensor("m_ps", [P, 2, HALF], F32))

        w_in = sem("w_in")
        ffw_in = sem("ffw_in")
        rows_in = sem("rows_in")
        const_step = sem("const_step")
        setup_step = sem("setup_step")
        unit_full = sem("unit_full")
        unit_free = sem("unit_free")
        idx_n_in = sem("idx_n_in")
        idx_f_in = sem("idx_f_in")
        xn_in = sem("xn_in")
        h2_in = sem("h2_in")
        r_step = sem("r_step")
        r_var = sem("r_var")
        r_sd = sem("r_sd")
        xn_ready = sem("xn_ready")
        absq_ready = sem("absq_ready")
        diag_ready = sem("diag_ready")
        fro_sq = sem("fro_sq")
        fro_ready = sem("fro_ready")
        fold_ready = sem("fold_ready")
        two_parts = sem("two_parts")
        part_ready = sem("part_ready")
        part_out = [sem(f"part_out{i}") for i in range(2)]
        staged = [sem(f"staged{i}") for i in range(2)]
        guard_set = sem("guard_set")
        row_scores = sem("row_scores")
        row_step = sem("row_step")
        row_parts = sem("row_parts")
        row_read = sem("row_read")
        gw_kept = sem("gw_kept")
        v_staged = sem("v_staged")
        s_full = sem("s_full")
        exp_done = sem("exp_done")
        pv_done = sem("pv_done")
        o_read = sem("o_read")
        sums_in = sem("sums_in")
        sums_inv = sem("sums_inv")
        inv_out = sem("inv_out")
        inv_in = sem("inv_in")
        o_norm = sem("o_norm")
        attn_in = sem("attn_in")
        h2_base = sem("h2_base")
        f_step = sem("f_step")
        f_var = sem("f_var")
        f_sd = sem("f_sd")
        xq_ready = sem("xq_ready")
        h2_b2 = sem("h2_b2")
        gelu_done = sem("gelu_done")
        gq_ready = sem("gq_ready")
        turn_full = sem("turn_full")
        turned = sem("turned")
        out_done = sem("out_done")
        passed_pool = sem("passed_pool")
        passed_dve = sem("passed_dve")
        passed_pe = sem("passed_pe")

        block = ctx.enter_context(nc.Block())

        def run(setup, items_of, slot, close, eng, inside=False):
            setup()

            def one_round(b, kind, base, attention=True):
                items, first, _ = kind
                for s in range(SLOTS):
                    def carried():
                        for it in items[s]:
                            items_of(it, b, base, first)

                    if attention and inside:
                        slot(b, s, kind, carried)
                    else:
                        if attention:
                            slot(b, s, kind)
                        carried()

            one_round(-1, ALONE, 0, attention=False)
            one_round(0, FIRST, BASE_0)
            with eng.Fori(1, B - 1) as b:
                one_round(b, BOTH, rounds(b))
            one_round(B - 1, LAST, rounds(B - 1))
            items_of(("load", 0), B, 0, {})
            close()
            one_round(B, TAIL, rounds(B - 1) + LAST[2], attention=False)

        @block.tensor
        def _(pe):
            def setup():
                pe.wait_ge(w_in, 16 * 4)
                pe.wait_ge(const_step, CONSTANTS)

            def turn(t):
                pe.wait_ge(gq_ready, (B - 1) * NT + t + 1)
                pe.wait_ge(exp_done, B * SLOTS * GH)
                if t >= 2:
                    pe.wait_ge(turned, t - 1)
                for k in range(HT):
                    last = nc.tensor.transpose(s_ps[:, t % 2, 0, :].bitcast(BF16)[:, k * P:(k + 1) * P],
                                               gq[:, t % 2, k * P:(k + 1) * P], ident_bf[:])
                last.then_inc(turn_full, 1)

            def items_of(it, b, base, first):
                name, arg = it
                if name == "turn":
                    turn(arg)
                if name not in UNITS_OF:
                    return
                local = first[it]
                u = base + local
                bank = m_ps[:, local % 2, :]
                beta = b + 1 if name in ("xT", "q", "k", "v", "qrow", "stat") else b - 1
                needs = {"q": ("xT", 3), "k": ("xT", 3), "v": ("xT", 3), "up": ("xqT", arg),
                         "down": ("gT", arg)}.get(name)
                if needs not in first:
                    needs = None
                pe.wait_ge(unit_free, base + max(local - 1, first[needs] + 1 if needs else 0))
                if name == "wsum":
                    pe.wait_ge(setup_step, FILLS + arg + 1)
                    nc.tensor.matmul(bank[:, 0:1], ones[:], w_abs[:, arg:arg + 1],
                                     start=True, stop=True).then_inc(unit_full, 1)
                elif name == "wT":
                    w, c = arg // 2, arg % 2
                    pe.wait_ge(setup_step, FILLS + 6 + 2 * w)
                    tiles = bank.bitcast(BF16).rearrange("p (j n) -> p j n", n=P)
                    for j in range(8):
                        if w == 0:
                            src = w1_bf[:, j * D + c * P:j * D + (c + 1) * P]
                        else:
                            src = w2_bf[:, c * HID + j * P:c * HID + (j + 1) * P]
                        last = nc.tensor.transpose(tiles[:, j, :], src, ident_bf[:])
                    last.then_inc(unit_full, 1)
                elif name == "xT":
                    dh, tg = arg // 2, arg % 2
                    pe.wait_ge(xn_ready, beta + 1)
                    for q in range(4):
                        last = nc.tensor.transpose(bank[:, q * P:(q + 1) * P],
                                                   xn[:, tg * 4 + q, dh * P:(dh + 1) * P], ident[:])
                    last.then_inc(unit_full, 1)
                elif name in ("q", "k"):
                    i, j = arg // 2, arg % 2
                    col = (0 if name == "q" else D) + i * P
                    for dh in range(DT):
                        last = nc.tensor.matmul(bank, wqkv[:, dh, col:col + P],
                                                xT[:, dh, j * HALF:(j + 1) * HALF],
                                                start=(dh == 0), stop=(dh == DT - 1))
                    last.then_inc(unit_full, 1)
                elif name == "v":
                    for r in range(2):
                        t = 2 * arg + r
                        for dh in range(DT):
                            last = nc.tensor.matmul(bank[:, r * D:(r + 1) * D],
                                                    xT[:, dh, t * P:(t + 1) * P],
                                                    wqkv[:, dh, 2 * D:3 * D],
                                                    start=(dh == 0), stop=(dh == DT - 1))
                    last.then_inc(unit_full, 1)
                elif name == "qrow":
                    pe.wait_ge(absq_ready, beta + 1)
                    for j in range(2):
                        r = 32 * (2 * arg + j)
                        last = nc.tensor.matmul(bank[r:r + 32, :], head_mask[:],
                                                absq[:, arg, j * HALF:(j + 1) * HALF],
                                                start=True, stop=True)
                    last.then_inc(unit_full, 1)
                elif name == "stat":
                    pe.wait_ge(diag_ready, 2 * beta + arg + 1)
                    nc.tensor.matmul(bank, ones[:],
                                     diag[:, 4 * arg:4 * arg + 4, :].rearrange("p c n -> p (c n)"),
                                     start=True, stop=True).then_inc(unit_full, 1)
                elif name == "proj":
                    pe.wait_ge(attn_in, (beta + 1) * 16 * GH * NG)
                    for k in range(DT):
                        last = nc.tensor.matmul(bank[:, 0:D], attn[:, k, arg * P:(arg + 1) * P],
                                                wp[:, k, :], start=(k == 0), stop=(k == DT - 1))
                    last.then_inc(unit_full, 1)
                elif name == "xqT":
                    pe.wait_ge(xq_ready, beta * NT + arg + 1)
                    view = bank.bitcast(BF16)
                    for k in range(DT):
                        last = nc.tensor.transpose(view[:, k * P:(k + 1) * P],
                                                   xq[:, arg % 2, k * P:(k + 1) * P], ident_bf[:])
                    last.then_inc(unit_full, 1)
                elif name == "up":
                    for c in range(2):
                        if c:
                            pe.wait_ge(unit_free, u)
                        for k in range(DT):
                            last = nc.tensor.matmul(m_ps[:, (local + c) % 2, :], xqT[:, arg % 2, k, :],
                                                    w1T[:, k, c * HALF:(c + 1) * HALF],
                                                    start=(k == 0), stop=(k == DT - 1))
                        last.then_inc(unit_full, 1)
                elif name == "gT":
                    pe.wait_ge(gq_ready, beta * NT + arg + 1)
                    view = bank.bitcast(BF16)
                    for k in range(HT):
                        last = nc.tensor.transpose(view[:, k * P:(k + 1) * P],
                                                   gq[:, arg % 2, k * P:(k + 1) * P], ident_bf[:])
                    last.then_inc(unit_full, 1)
                elif name == "down":
                    if ("gT", arg) not in first:
                        pe.wait_ge(turned, arg + 1)
                    for k in range(HT):
                        last = nc.tensor.matmul(bank[:, 0:D], gqT[:, arg % 2, k, :], w2T[:, k, :],
                                                start=(k == 0), stop=(k == HT - 1))
                    last.then_inc(unit_full, 1)

            def pv_half(b, s, half):
                g, j = s // NT, s % NT
                for hh in range(GH):
                    last = nc.tensor.matmul(o_ps[32 * hh:32 * hh + 32, half, :],
                                            vs[g % 2][:, j, hh, :],
                                            probs[:, s % 2, hh, half * HALF:(half + 1) * HALF],
                                            start=(j == 0), stop=(j == NT - 1))
                if half == 1:
                    last.then_inc(pv_done, 1)

            def pv_waits(b, s):
                g, j = s // NT, s % NT
                pe.wait_ge(exp_done, (b * SLOTS + s + 1) * GH)
                if j == 0:
                    pe.wait_ge(v_staged, b * NG + g + 1)
                    if g > 0 or not (starts(b, 0)):
                        pe.wait_ge(o_read, b * NG + g)

            def row_maxima(b, g, units):
                with pe.If(pe_wide["now"]):
                    pe.wait_ge(staged[g % 2], (b * 2 + g // 2 + 1) * 16 * 9)
                    pe.wait_ge(unit_free, units)
                    pass_wait(pe, passed_pe)
                    for hh in range(GH):
                        with pe.Fori(0, NT) as t:
                            k = ((b * NG + g) * GH + hh) * NT + t
                            pe.wait_ge(row_read, 2 * k)
                            for half in range(2):
                                last = nc.tensor.matmul(m_ps[:, half, :],
                                                        qh[g % 2][0:GUARD, hh, bass.ds(t * P, P)],
                                                        kh[g % 2][0:GUARD, hh, half * HALF:(half + 1) * HALF],
                                                        start=True, stop=True)
                            last.then_inc(row_scores, 1)
                            pe.wait_ge(row_parts, k + 1)
                            nc.tensor.transpose(m_ps[:, 0, :].bitcast(BF16)[:, 0:P], top_parts[:],
                                                ident_bf[:]).then_inc(row_scores, 1)
                    pe.wait_ge(row_read, 2 * (b * NG + g + 1) * GH * NT)
                with pe.Else():
                    pe.sem_inc(row_scores, 2 * GH * NT)

            pe_wide = {}

            def slot(b, s, kind, carried):
                g, j = s // NT, s % NT
                before_b = b * BOTH[2] + (BASE_1 - BOTH[2]) if not starts(b, 0) else BASE_0
                if s == 0:
                    pe.wait_ge(fold_ready, b + 1)
                    pass_wait(pe, passed_pe)
                    pe_wide["now"] = pe.value_load(wide[0:1, 0:1], min_val=0, max_val=1)
                    row_maxima(b, 0, before_b)
                if j == 0:
                    pe.wait_ge(staged[g % 2], (b * 2 + g // 2 + 1) * 16 * 9)
                    pe.wait_ge(guard_set, b * NG + g + 1)
                where = 1 if s > 0 and any(it[0] == "gelu" for it in kind[0][s - 1]) else 2
                for hh in range(GH):
                    n = GH * s + hh
                    if n >= 2 or not (starts(b, 0)):
                        pe.wait_ge(exp_done, b * SLOTS * GH + n - 1)
                    for half in range(2):
                        last = nc.tensor.matmul(s_ps[:, n % 2, half, :],
                                                kh[g % 2][:, hh, j * P:(j + 1) * P],
                                                qh[g % 2][:, hh, half * HALF:(half + 1) * HALF],
                                                start=True, stop=True)
                    last.then_inc(s_full, 1)
                    if hh % 2 and (s > 0 or not starts(b, 0)):
                        before = (b, s - 1) if s > 0 else (b - 1, SLOTS - 1)
                        if hh == 1:
                            pv_waits(*before)
                        pv_half(*before, hh // 2)
                    if hh == where:
                        if j == 0 and g + 1 < NG:
                            row_maxima(b, g + 1, before_b + units_before(kind, s))
                        carried()

            def close():
                pv_waits(B - 1, SLOTS - 1)
                pv_half(B - 1, SLOTS - 1, 0)
                pv_half(B - 1, SLOTS - 1, 1)

            run(setup, items_of, slot, close, pe, inside=True)

        @block.scalar
        def _(act):
            def setup():
                act.dma_start(wqkv[:], w_qkv.rearrange("(k p) n -> p k n", p=P)).then_inc(w_in, 16)
                act.dma_start(wp[:], w_proj.rearrange("(k p) n -> p k n", p=P)).then_inc(w_in, 16)
                act.dma_start(bqk[:, 0:2], b_qkv[0:D].rearrange("(i p) -> p i", p=P),
                              allow_slow_non_contiguous=True).then_inc(w_in, 16)
                act.dma_start(bqk[:, 2:4], b_qkv[D:2 * D].rearrange("(i p) -> p i", p=P),
                              allow_slow_non_contiguous=True).then_inc(w_in, 16)

            def items_of(it, b, base, first):
                name, arg = it
                if name == "diag":
                    beta = b + 1
                    act.wait_ge(unit_free, base + first[("k", 3)] + 1)
                    if not starts(beta, 0):
                        for ring in range(2):
                            act.wait_ge(part_out[ring], beta * 2 * 3 * 16)
                    nc.scalar.activation(absq[:].rearrange("p i n -> p (i n)"),
                                         qk[:, 0, :, :].rearrange("p i n -> p (i n)"), ACT.Abs)\
                        .then_inc(absq_ready, 1)
                elif name == "gelu":
                    for t in arg:
                        act.wait_ge(unit_free, base + first[("up", t)] + 2)
                        nc.scalar.activation(hid[:, t % 4, :], hid[:, t % 4, :], ACT.Gelu).then_inc(gelu_done, 1)

                elif name == "turn":
                    act.wait_ge(turn_full, arg + 1)
                    if arg >= 2:
                        act.wait_ge(unit_full, base + first[("down", arg - 2)] + 1)
                    nc.scalar.copy(gqT[:, arg % 2, :, :].rearrange("p k n -> p (k n)"),
                                   s_ps[:, arg % 2, 0, :].bitcast(BF16)).then_inc(turned, 1)

            def slot(b, s, kind):
                for hh in range(GH):
                    n = GH * s + hh
                    act.wait_ge(s_full, b * SLOTS * GH + n + 1)
                    if hh == 0 and (s >= 2 or not (starts(b, 0))):
                        act.wait_ge(pv_done, b * SLOTS + s - 1)
                    nc.scalar.activation(probs[:, s % 2, hh, :],
                                         s_ps[:, n % 2, :, :].rearrange("p a n -> p (a n)"),
                                         ACT.Exp).then_inc(exp_done, 1)
                if s % NT == 0:
                    if s > 0:
                        take_o(b, s // NT - 1)
                    elif not starts(b, 0):
                        take_o(b - 1, NG - 1)

            def take_o(b, g):
                act.wait_ge(pv_done, b * SLOTS + (g + 1) * NT)
                if g > 0 or not starts(b, 0):
                    act.wait_ge(attn_in, (b * NG + g) * 16 * GH)
                nc.scalar.copy(o_sb[:], o_ps[:].rearrange("p a n -> p (a n)")).then_inc(o_read, 1)

            run(setup, items_of, slot, lambda: take_o(B - 1, NG - 1), act)

        @block.sync
        def _(sp):
            def setup():
                sp.dma_start(idx_n[:], x_v[0]).then_inc(idx_n_in, 16)
                for r in range(2):
                    sp.dma_start(bv[:, r, :], b_qkv[2 * D:3 * D].partition_broadcast(P)).then_inc(rows_in, 16)
                sp.dma_start(bp[:], b_proj.partition_broadcast(P)).then_inc(rows_in, 16)
                sp.dma_start(b1_row[:], b1.partition_broadcast(P)).then_inc(rows_in, 16)
                sp.dma_start(b2_row[:], b2.partition_broadcast(P)).then_inc(rows_in, 16)

            def stage(b, g):
                later = g >= 2 or not (starts(b, 0))
                if later:
                    sp.wait_ge(s_full, (b * NG + g - 1) * NT * GH)
                if g % 2 == 0:
                    for ring in range(2):
                        sp.wait_ge(part_out[ring], (b * 2 + g // 2 + 1) * 3 * 16)
                hs = slice(g * GH, (g + 1) * GH)
                for t0, n in K_RUNS:
                    sp.dma_start(kh[g % 2][t0 * HD:(t0 + n) * HD, :, :],
                                 parts_dram[1, hs, 0:n, :, :].rearrange("h c d n -> (c d) h n"))\
                      .then_inc(staged[g % 2], 16)
                for t, c in enumerate(Q_PART):
                    sp.dma_start(qh[g % 2][t * HD:(t + 1) * HD, :, :],
                                 parts_dram[0, hs, c, :, :].rearrange("h d n -> d h n"))\
                      .then_inc(staged[g % 2], 16)

            def invert(b, g):
                n = b * NG + g + 1
                sp.wait_ge(o_read, n)
                sp.dma_start(sums[:], o_sb[HD:P:32, :]).then_inc(sums_in, 16)
                sp.wait_ge(sums_inv, n)
                sp.dma_start(inv_dram.rearrange("h (a c) -> (h a) c", c=GH * N // P), sums[:])\
                  .then_inc(inv_out, 16)
                sp.wait_ge(inv_out, n * 16)
                for hh in range(GH):
                    sp.dma_start(o_div[32 * hh:32 * hh + HD, :], inv_dram[hh, :].partition_broadcast(HD))\
                      .then_inc(inv_in, 16)

            def attn_rows(b, g):
                sp.wait_ge(o_norm, b * NG + g + 1)
                if g == 0 and not starts(b, 0):
                    sp.wait_ge(unit_full, last_proj(b))
                for hh in range(GH):
                    r = (g % 2) * GH * HD + hh * HD
                    sp.dma_start(attn[r:r + HD, g // 2, :], o_sb[32 * hh:32 * hh + HD, :])\
                      .then_inc(attn_in, 16)

            def last_proj(b):
                kind = LAST if isinstance(b, int) else BOTH
                return rounds(b) + kind[1][("proj", NT - 1)] + 1

            def items_of(it, b, base, first):
                name, arg = it
                if name == "wload":
                    sp.dma_start(w1_raw.rearrange("p (j d) -> p j d", d=D),
                                 w1.rearrange("(j p) d -> p j d", p=P)).then_inc(ffw_in, 16)
                    sp.dma_start(w2_raw.rearrange("p (c n) -> p c n", n=HID),
                                 w2.rearrange("(c p) n -> p c n", p=P)).then_inc(ffw_in, 16)
                elif name == "stats":
                    sp.wait_ge(xn_in, (b + 2) * 16 * NT)
                    sp.dma_start(idx_n[:], x_v[(b + 2) % B]).then_inc(idx_n_in, 16)
                elif name == "split":
                    which, i = arg
                    beta = b + 1
                    w = 0 if which == "q" else 1
                    n = SPLITS.index(arg)
                    sp.wait_ge(part_ready, beta * 4 + n + 1)
                    if n % 2 == 0 and not (starts(b, -1)):
                        for ring in range(2):
                            sp.wait_ge(staged[ring], (beta * 2 - 1 + i) * 16 * 9)
                    for c in range(3):
                        sp.dma_start(parts_dram[w, i * HPT:(i + 1) * HPT, c, :, :], part[:, n % 2, c, :])\
                          .then_inc(part_out[n % 2], 16)
                elif name == "stage":
                    stage(b + 1, 0)
                elif name == "store":
                    beta = b - 1
                    sp.wait_ge(unit_free, base + first[("down", NT - 1)] + 1)
                    sp.dma_start(out_v[beta], h2[:]).then_inc(out_done, 16)

            def tokens_again(b):
                if not (starts(b, 1)):
                    sp.wait_ge(h2_in, (b - 1) * 16 * NT)
                sp.dma_start(idx_f[:], x_v[b - 1]).then_inc(idx_f_in, 16)

            def slot(b, s, kind):
                g = s // NT
                if s == 0 and not starts(b, 0):
                    tokens_again(b)
                if s % NT == 0 and g + 1 < NG:
                    stage(b, g + 1)
                elif s % NT == 1:
                    if s > 1:
                        before = b, g - 1
                    elif not starts(b, 0):
                        before = b - 1, NG - 1
                    else:
                        return
                    invert(*before)
                    attn_rows(*before)

            def close():
                tokens_again(B)
                invert(B - 1, NG - 1)
                attn_rows(B - 1, NG - 1)

            run(setup, items_of, slot, close, sp)
            sp.wait_ge(out_done, 16 * B)

        @block.gpsimd
        def _(pool):
            def setup():
                pool.wait_ge(idx_n_in, 16)
                gather(xn, idx_n, xn_in)
                step = Chain(pool, const_step, 0)
                step.inc(nc.gpsimd.memset(ones[:], 1.0))
                step.inc(nc.gpsimd.memset(ident[:], 0.0))
                step.inc(nc.gpsimd.memset(head_mask[:], 0.0))
                step.inc(nc.gpsimd.memset(guard_mask[:], 0.0))
                step.inc(nc.gpsimd.memset(half_c[:], 0.5))
                step.wait()
                step.inc(nc.gpsimd.affine_select(out=ident[:], in_=ident[:], compare_op=ALU.not_equal,
                                                 fill=1.0, base=0, pattern=[[-1, P]],
                                                 channel_multiplier=1))
                step.inc(nc.gpsimd.affine_select(out=guard_mask[:], in_=guard_mask[:],
                                                 compare_op=ALU.not_equal, fill=1.0, base=-GUARD,
                                                 pattern=[[-1, 3]], channel_multiplier=1))
                step.inc(nc.gpsimd.affine_select(out=head_mask[:, 0:HPT], in_=ones[:, 0:HPT],
                                                 compare_op=ALU.is_ge, fill=0.0, base=0,
                                                 pattern=[[-HD, HPT]], channel_multiplier=1))
                step.wait()
                step.inc(nc.gpsimd.affine_select(out=head_mask[:, 0:HPT], in_=head_mask[:, 0:HPT],
                                                 compare_op=ALU.is_ge, fill=0.0, base=HD - 1,
                                                 pattern=[[HD, HPT]], channel_multiplier=-1))
                step.inc(nc.gpsimd.tensor_copy(ident_bf[:], ident[:]))
                step.wait()

            def gather(dst, idx, sem_in):
                pass_wait(pool, passed_pool)
                for t in range(NT):
                    nc.gpsimd.indirect_dma_start(
                        out=dst[:, t, :], out_offset=None, in_=table,
                        in_offset=bass.IndirectOffsetOnAxis(ap=idx[:, t:t + 1], axis=0)).then_inc(sem_in, 16)

            def root(var, root_out, sem_var, sem_root, beta):
                pool.wait_ge(sem_var, beta + 1)
                pass_wait(pool, passed_pool)
                nc.gpsimd.tensor_scalar(root_out[:], var, EPS, None, ALU.add).then_inc(sem_root, 1)
                pool.wait_ge(sem_root, 2 * beta + 1)
                nc.gpsimd.tensor_tensor(root_out[:], root_out[:], half_c[:, 0:NT], ALU.pow).then_inc(sem_root, 1)

            def items_of(it, b, base, first):
                name, arg = it
                if name == "gather":
                    pool.wait_ge(idx_n_in, (b + 3) * 16)
                    pool.wait_ge(unit_free, base + first[("xT", 3)] + 1)
                    gather(xn, idx_n, xn_in)
                elif name == "stats":
                    beta = b + 1
                    root(mv[:, :, 1], sd, r_var, r_sd, beta)
                elif it == ("stat", 0):
                    beta = b + 1
                    pool.wait_ge(fro_sq, beta + 1)
                    nc.gpsimd.tensor_tensor(st[:, FRO, :], st[:, FRO2, :], half_c[:, 0:H], ALU.pow)\
                        .then_inc(fro_ready, 1)
                elif name == "split":
                    n, beta = SPLITS.index(arg), b + 1
                    pool.wait_ge(two_parts, beta * 4 + n + 1)
                    nc.gpsimd.tensor_tensor(part[:, n % 2, 2, :], rest, part[:, n % 2, 1, :],
                                            ALU.subtract).then_inc(part_ready, 1)
                elif name == "v" and arg == 3:
                    if starts(b, -1):
                        pool.wait_ge(setup_step, FILLS)
                    pool.wait_ge(unit_free, base + first[it] + 1)
                    stage(b + 1, 0)
                elif name == "load":
                    beta = b - 1
                    pool.wait_ge(idx_f_in, (beta + 1) * 16)
                    if not (starts(b, 1)):
                        pool.wait_ge(out_done, beta * 16)
                    gather(h2, idx_f, h2_in)
                elif name == "base":
                    beta = b - 1
                    pool.wait_ge(h2_in, (beta + 1) * 16 * NT)
                    if starts(b, 1):
                        pool.wait_ge(rows_in, 16 * 5)
                    nc.gpsimd.tensor_tensor(h2[:], h2[:], bp[:].unsqueeze(1).to_broadcast([P, NT, D]),
                                            ALU.add).then_inc(h2_base, 1)
                elif name == "rstd":
                    root(mv2[:, :, 1], sd2, f_var, f_sd, b - 1)
                elif name == "xq":
                    pool.wait_ge(xq_ready, (b - 1) * NT + arg + 1)
                    nc.gpsimd.tensor_tensor(h2[:, arg, :], h2[:, arg, :], b2_row[:], ALU.add).then_inc(h2_b2, 1)

            def stage(b, g):
                if g >= 2 or not starts(b, 0):
                    pool.wait_ge(pv_done, (b * NG + g - 1) * NT)
                pass_wait(pool, passed_pool)
                nc.gpsimd.tensor_copy(vs[g % 2][:, :, :, 0:HD],
                                      vn[:, :, g * GH * HD:(g + 1) * GH * HD]
                                      .rearrange("p t (h d) -> p t h d", d=HD)).then_inc(v_staged, 1)

            def normalise(b, g):
                pool.wait_ge(inv_in, (b * NG + g + 1) * 16 * GH)
                nc.gpsimd.tensor_tensor(o_sb[:], o_sb[:], o_div[:], ALU.mult).then_inc(o_norm, 1)

            def slot(b, s, kind):
                g = s // NT
                if s % NT == 1:
                    if g + 1 < NG:
                        stage(b, g + 1)
                elif s % NT == 3:
                    if s > 3:
                        normalise(b, g - 1)
                    elif not starts(b, 0):
                        normalise(b - 1, NG - 1)

            def close():
                normalise(B - 1, NG - 1)

            run(setup, items_of, slot, close, pool)

        @block.vector
        def _(dve):
            V = nc.vector

            def setup():
                step = Chain(dve, setup_step, 0)
                for i in range(2):
                    step.inc(V.memset(kh[i][GUARD:P, :, :], 1.0))
                    step.inc(V.memset(vs[i][:], 0.0))
                step.inc(V.memset(o_div[:], 1.0))
                step.inc(V.memset(top_parts[:], 0.0))
                step.wait()
                for i in range(2):
                    step.inc(V.memset(vs[i][:, :, :, HD:HD + 1], 1.0))
                step.wait()
                dve.wait_ge(const_step, CONSTANTS)

            chains = {}

            def items_of(it, b, base, first):
                name, arg = it
                bank = None
                if name in UNITS_OF:
                    dve.wait_ge(unit_full, base + first[it] + 1)
                    bank = m_ps[:, first[it] % 2, :]
                if name == "stats":
                    chains["R"] = Chain(dve, r_step, (b + 1) * R_STEPS)
                elif name == "load":
                    chains["F"] = Chain(dve, f_step, (b - 1) * F_STEPS)
                if name in W_NAMES:
                    weights(it, base, first, bank)
                elif any(it in R_ITEMS[s] for s in range(SLOTS)):
                    prepare(it, b + 1, base, first, bank, chains["R"])
                else:
                    feed_forward(it, b - 1, base, first, bank, chains["F"])

            def weights(it, base, first, bank):
                name, arg = it
                raws, terns = (w1_raw, w2_raw), (w1_bf, w2_bf)
                if name == "wabs":
                    dve.wait_ge(ffw_in, 32)
                    for w in range(2):
                        V.tensor_reduce(w_abs[:, w:w + 1], raws[w], AX.X, ALU.add,
                                        apply_absolute_value=True).then_inc(setup_step, 1)
                elif name == "wsum":
                    V.tensor_scalar(w_scale[:, arg:arg + 1], bank[:, 0:1], 1.0 / (HID * D), EPS,
                                    ALU.mult, ALU.max).then_inc(unit_free, 1)
                    if arg == 1:
                        dve.wait_ge(unit_free, base + first[it] + 1)
                        for c, half in enumerate((0.5, -0.5)):
                            V.tensor_scalar(w_half[:, 2 * c:2 * c + 2], w_scale[:], half, None, ALU.mult)\
                             .then_inc(setup_step, 1)
                elif name == "tern":
                    dve.wait_ge(setup_step, FILLS + 4 + 2 * arg)
                    V.tensor_scalar(terns[arg], raws[arg], w_half[:, 2 + arg:3 + arg], None, ALU.is_lt)\
                     .then_inc(setup_step, 1)
                    dve.wait_ge(setup_step, FILLS + 5 + 2 * arg)
                    V.scalar_tensor_tensor(out=terns[arg], in0=raws[arg], scalar=w_half[:, arg:arg + 1],
                                           in1=terns[arg], op0=ALU.is_gt, op1=ALU.subtract)\
                     .then_inc(setup_step, 1)
                elif name == "wT" and arg < 2:
                    V.tensor_copy(w1T[:, arg, :], bank.bitcast(BF16)).then_inc(unit_free, 1)
                elif name == "wT":
                    c = arg - 2
                    V.tensor_copy(w2T[:, :, c * P:(c + 1) * P],
                                  bank.bitcast(BF16).rearrange("p (j n) -> p j n", n=P))\
                     .then_inc(unit_free, 1)

            def prepare(it, beta, base, first, bank, step):
                name, arg = it
                if name == "stats":
                    dve.wait_ge(xn_in, (beta + 1) * 16 * NT)
                    for t in range(NT):
                        step.inc(V.bn_stats(bst[:, t, :], xn[:, t, :]))
                    step.wait()
                    pass_wait(dve, passed_dve)
                    for t in range(NT):
                        last = V.bn_aggr(mv[:, t, :], bst[:, t, :])
                    last.then_inc(r_var, 1)
                elif name == "norm":
                    dve.wait_ge(r_sd, 2 * (beta + 1))
                    step.inc(V.reciprocal(sd[:], sd[:]))
                    step.wait()
                    for t in range(NT):
                        last = V.tensor_scalar(xn[:, t, :], xn[:, t, :], mv[:, t, 0:1], sd[:, t:t + 1],
                                               ALU.subtract, ALU.mult)
                    last.then_inc(xn_ready, 1)
                elif name == "xT":
                    dh, tg = arg // 2, arg % 2
                    if arg == 0 and starts(beta, 0):
                        dve.wait_ge(w_in, 16 * 4)
                        dve.wait_ge(rows_in, 16 * 5)
                    V.tensor_copy(xT[:, dh, tg * HALF:(tg + 1) * HALF], bank).then_inc(unit_free, 1)
                elif name == "xsum":
                    dve.wait_ge(unit_free, base + first[("xT", 3)] + 1)
                    for dh in range(DT):
                        step.inc(V.tensor_reduce(pair[:, dh:dh + 1], xT[:, dh, :], AX.X, ALU.add,
                                                 apply_absolute_value=True))
                    step.wait()
                    step.inc(V.tensor_tensor(stat[:, 6:7], pair[:, 0:1], pair[:, 1:2], ALU.max))
                elif name in ("q", "k"):
                    i, j = arg // 2, arg % 2
                    w = 0 if name == "q" else 1
                    V.tensor_scalar(qk[:, w, i, j * HALF:(j + 1) * HALF], bank,
                                    bqk[:, 2 * w + i:2 * w + i + 1], None, ALU.add).then_inc(unit_free, 1)
                elif name == "v":
                    if arg == 0 and not starts(beta, 0):
                        dve.wait_ge(v_staged, beta * NG)
                    V.tensor_tensor(vn[:, 2 * arg:2 * arg + 2, :],
                                    bank.rearrange("p (r d) -> p r d", r=2), bv[:], ALU.add)\
                        .then_inc(unit_free, 1)
                elif name == "sq":
                    dve.wait_ge(unit_free, base + first[("q", 2 * arg + 1)] + 1)
                    step.wait()
                    step.inc(V.tensor_tensor_reduce(out=rest, in0=qk[:, 0, arg, :], in1=qk[:, 0, arg, :],
                                                    scale=1.0, scalar=0.0, op0=ALU.mult, op1=ALU.add,
                                                    accum_out=stat[:, arg:arg + 1]))
                elif name == "sk":
                    dve.wait_ge(unit_free, base + first[("k", 2 * arg + 1)] + 1)
                    step.inc(V.tensor_reduce(stat[:, 2 + arg:3 + arg], qk[:, 1, arg, :], AX.X, ALU.add,
                                             apply_absolute_value=True))
                    step.inc(V.tensor_reduce(stat[:, 4 + arg:5 + arg], qk[:, 1, arg, :], AX.X, ALU.max,
                                             apply_absolute_value=True))
                elif name == "diag":
                    step.wait()
                    for c in range(4):
                        last = V.tensor_scalar(diag[:, c, :], ident[:], stat[:, c:c + 1], None, ALU.mult)
                    last.then_inc(diag_ready, 1)
                elif name == "qrow":
                    r = 64 * arg
                    V.tensor_reduce(stat[r:r + 64, 7:8], bank[r:r + 64, :], AX.X, ALU.max)\
                        .then_inc(unit_free, 1)
                    if arg == 1:
                        dve.wait_ge(unit_free, base + first[it] + 1)
                        step.wait()
                        for c in range(4, 8):
                            last = V.tensor_scalar(diag[:, c, :], ident[:], stat[:, c:c + 1], None, ALU.mult)
                        last.then_inc(diag_ready, 1)
                elif name == "stat":
                    by_head = [bank[:, c * D:(c + 1) * D].rearrange("p (h d) -> p h d", d=HD) for c in range(2)]
                    if arg == 0:
                        V.tensor_reduce(st[:, FRO2, :], by_head[0], AX.X, ALU.add).then_inc(fro_sq, 1)
                        V.tensor_reduce(st[:, K_SUM, :], by_head[1], AX.X, ALU.max).then_inc(unit_free, 1)
                    else:
                        step.inc(V.tensor_reduce(st[:, K_MAX, :], by_head[0], AX.X, ALU.max))
                        step.inc(V.tensor_reduce(st[:, X_SUM, 0:1], bank[:, D:D + P], AX.X, ALU.max))
                        rows = bank[:, D + P:2 * D].rearrange("p (i j r) -> p i r j", i=DT, j=2)
                        V.tensor_reduce(st[:, Q_SUM, :].rearrange("p (i r) -> p i r", i=DT),
                                        rows[:, :, 0:HPT, :], AX.X, ALU.max).then_inc(unit_free, 1)
                elif name == "fold":
                    fold(beta, base, first, step)
                elif name == "split":
                    which, i = arg
                    n = SPLITS.index(arg)
                    src = qk[:, 0 if which == "q" else 1, i, :]
                    if n >= 2:
                        dve.wait_ge(part_out[n % 2], (beta * 2 + 1) * 3 * 16)
                    if which == "q":
                        step.inc(V.tensor_scalar(src, src, scol[:, i:i + 1], None, ALU.mult))
                        step.wait()
                    step.inc(V.tensor_copy(part[:, n % 2, 0, :], src))
                    step.wait()
                    if n:
                        dve.wait_ge(part_ready, beta * 4 + n)
                    step.inc(V.tensor_tensor(rest, src, part[:, n % 2, 0, :], ALU.subtract))
                    step.wait()
                    V.tensor_copy(part[:, n % 2, 1, :], rest).then_inc(two_parts, 1)
                    if n == 3:
                        assert step.n == R_STEPS, step.n
                elif name == "stage":
                    set_guard(beta, 0)

            def fold(beta, base, first, step):
                def op(ins):
                    step.inc(ins)
                    step.wait()

                dve.wait_ge(unit_free, base + first[("stat", 1)] + 1)
                dve.wait_ge(fro_ready, beta + 1)
                op(V.tensor_scalar(st[:, DENOM, :], st[:, FRO, :], st[:, X_SUM, 0:1], None, ALU.mult))
                op(V.reciprocal(st[:, DENOM, :], st[:, DENOM, :]))
                step.inc(V.tensor_scalar(st[:, TWICE, :], st[:, DENOM, :], 2.0, None, ALU.mult))
                step.inc(V.tensor_tensor(st[:, SHIFT, :], st[:, Q_SUM, :], st[:, K_MAX, :], ALU.mult))
                step.inc(V.tensor_tensor(st[:, K_SUM, :], st[:, K_SUM, :], st[:, K_SUM, :], ALU.mult))
                op(V.tensor_tensor(st[:, Q_SUM, :], st[:, Q_SUM, :], st[:, Q_SUM, :], ALU.mult))
                step.inc(V.tensor_tensor(st[:, SHIFT, :], st[:, SHIFT, :], st[:, TWICE, :], ALU.mult))
                op(V.tensor_tensor(st[:, CONST, :], st[:, Q_SUM, :], st[:, K_SUM, :], ALU.add))
                op(V.tensor_reduce(bound[:], st[:, SHIFT, :], AX.X, ALU.max))
                step.inc(V.tensor_scalar(wide[:], bound[:], LIMIT, None, ALU.is_gt))
                op(V.scalar_tensor_tensor(out=st[:, CONST, :], in0=st[:, CONST, :], scalar=-1.0,
                                          in1=st[:, DENOM, :], op0=ALU.mult, op1=ALU.mult))
                op(V.tensor_tensor(st[:, SHIFT, :], st[:, SHIFT, :], st[:, CONST, :], ALU.add))
                op(V.tensor_tensor(gtmp[:], st[:, CONST, :], st[:, SHIFT, :], ALU.subtract))
                op(V.tensor_copy(gpart[:, 0, :], gtmp[:]))
                op(V.tensor_tensor(gtmp[:], gtmp[:], gpart[:, 0, :], ALU.subtract))
                op(V.tensor_copy(gpart[:, 1, :], gtmp[:]))
                op(V.tensor_tensor(gpart[:, 2, :], gtmp[:], gpart[:, 1, :], ALU.subtract))
                op(V.tensor_scalar(gsel[:], gpart[:, 0, :], guard_mask[:, 0:1], None, ALU.mult))
                op(V.scalar_tensor_tensor(out=gsel[:], in0=gpart[:, 1, :], scalar=guard_mask[:, 1:2],
                                          in1=gsel[:], op0=ALU.mult, op1=ALU.add))
                op(V.tensor_tensor(smul[:], head_mask[:, 0:HPT].unsqueeze(1).to_broadcast([P, DT, HPT]),
                                   st[:, TWICE, :].rearrange("p (i h) -> p i h", i=DT), ALU.mult))
                op(V.tensor_reduce(scol[:], smul[:], AX.X, ALU.add))
                if not starts(beta, 0):
                    dve.wait_ge(guard_set, beta * NG - 1)
                V.scalar_tensor_tensor(out=gw[:], in0=gpart[:, 2, :], scalar=guard_mask[:, 2:3],
                                       in1=gsel[:], op0=ALU.mult, op1=ALU.add).then_inc(fold_ready, 1)

            def quantise(step, src, scales, w, dst, ready):
                def op(ins):
                    step.inc(ins)
                    step.wait()

                op(V.tensor_reduce(scales[:, 0:1], src, AX.X, ALU.max, apply_absolute_value=True))
                op(V.tensor_scalar(scales[:, 1:2], scales[:, 0:1], EPS, 1.0 / QB, ALU.max, ALU.mult))
                op(V.reciprocal(scales[:, 2:3], scales[:, 1:2]))
                step.inc(V.tensor_scalar(scales[:, 3:4], scales[:, 1:2], w_scale[:, w:w + 1], None, ALU.mult))
                op(V.tensor_scalar(src, src, scales[:, 2:3], MAGIC, ALU.mult, ALU.add))
                V.tensor_scalar(dst, src, -MAGIC, QB, ALU.add, ALU.min).then_inc(ready, 1)

            def feed_forward(it, beta, base, first, bank, step):
                name, t = it
                if name == "proj":
                    if t == 0:
                        dve.wait_ge(h2_base, beta + 1)
                    V.tensor_tensor(h2[:, t, :], bank[:, 0:D], h2[:, t, :], ALU.add).then_inc(unit_free, 1)
                    dve.wait_ge(unit_free, base + first[it] + 1)
                    step.inc(V.bn_stats(bst2[:, t, :], h2[:, t, :]))
                    step.wait()
                    pass_wait(dve, passed_dve)
                    aggr = V.bn_aggr(mv2[:, t, :], bst2[:, t, :])
                    if t == NT - 1:
                        aggr.then_inc(f_var, 1)
                    else:
                        step.inc(aggr)
                elif name == "rstd":
                    dve.wait_ge(f_sd, 2 * (beta + 1))
                    step.inc(V.reciprocal(sd2[:], sd2[:]))
                elif name == "xq":
                    step.wait()
                    if t > 0 or not starts(beta, 0):
                        dve.wait_ge(xq_ready, beta * NT + t)
                    step.inc(V.tensor_scalar(xf[:], h2[:, t, :], mv2[:, t, 0:1], sd2[:, t:t + 1],
                                             ALU.subtract, ALU.mult))
                    step.wait()
                    quantise(step, xf[:], sx[:, t, :], 0, xq[:, t % 2, :], xq_ready)
                elif name == "xqT":
                    V.tensor_copy(xqT[:, t % 2, :, :].rearrange("p k n -> p (k n)"),
                                  bank.bitcast(BF16)[:, 0:D]).then_inc(unit_free, 1)
                elif name == "up":
                    step.wait()
                    for c in range(2):
                        u = base + first[it] + c
                        dve.wait_ge(unit_full, u + 1)
                        V.scalar_tensor_tensor(out=hid[:, t % 4, c * HALF:(c + 1) * HALF],
                                               in0=m_ps[:, (first[it] + c) % 2, :], scalar=sx[:, t, 3:4],
                                               in1=b1_row[:, c * HALF:(c + 1) * HALF],
                                               op0=ALU.mult, op1=ALU.add).then_inc(unit_free, 1)
                elif name == "gq":
                    if ("gT", t) not in first and t >= 2:
                        dve.wait_ge(turned, t - 1)
                    dve.wait_ge(gelu_done, beta * NT + t + 1)
                    quantise(step, hid[:, t % 4, :], sg[:, t, :], 1, gq[:, t % 2, :], gq_ready)
                elif name == "gT":
                    V.tensor_copy(gqT[:, t % 2, :, :].rearrange("p k n -> p (k n)"),
                                  bank.bitcast(BF16)).then_inc(unit_free, 1)
                elif name == "down":
                    step.wait()
                    dve.wait_ge(h2_b2, beta * NT + t + 1)
                    V.scalar_tensor_tensor(out=h2[:, t, :], in0=bank[:, 0:D], scalar=sg[:, t, 3:4],
                                           in1=h2[:, t, :], op0=ALU.mult, op1=ALU.add)\
                        .then_inc(unit_free, 1)
                    if t == NT - 1:
                        assert step.n == F_STEPS, step.n

            def invert(b, g):
                dve.wait_ge(sums_in, (b * NG + g + 1) * 16)
                V.reciprocal(sums[:], sums[:]).then_inc(sums_inv, 1)

            def set_guard(b, g):
                later = g >= 2 or not starts(b, 0)
                rows = gw[:, g * GH:(g + 1) * GH]
                if g == 0:
                    dve.wait_ge(fold_ready, b + 1)
                elif g == NG - 1:
                    dve.wait_ge(gw_kept, b + 1)
                    rows = gw_last
                if later:
                    dve.wait_ge(s_full, (b * NG + g - 1) * NT * GH)
                if g == NG - 2:
                    V.tensor_copy(gw_last[:], gw[:, (NG - 1) * GH:]).then_inc(gw_kept, 1)
                for hh in range(GH):
                    last = V.tensor_scalar(qh[g % 2][GUARD:P, hh, :], kh[g % 2][GUARD:P, hh, :],
                                           rows[GUARD:P, hh:hh + 1], None, ALU.mult)
                last.then_inc(guard_set, 1)

            dve_wide = {}

            def row_maxima(b, g):
                with dve.If(dve_wide["now"]):
                    dve.wait_ge(guard_set, b * NG + g + 1)
                    pass_wait(dve, passed_dve)
                    for hh in range(GH):
                        with dve.Fori(0, NT) as t:
                            k = ((b * NG + g) * GH + hh) * NT + t
                            dve.wait_ge(row_scores, 2 * k + 1)
                            V.tensor_reduce(top[:, 0:1], m_ps[:].rearrange("p a n -> p (a n)"),
                                            AX.X, ALU.max).then_inc(row_read, 1)
                            dve.wait_ge(row_read, 2 * k + 1)
                            step = Chain(dve, row_step, k * 4)
                            step.inc(V.tensor_scalar(top[:, 0:1], top[:, 0:1], -1.0, None, ALU.mult))
                            step.wait()
                            step.inc(V.tensor_copy(top_parts[:, GUARD:GUARD + 1], top[:, 0:1]))
                            step.wait()
                            step.inc(V.tensor_tensor(top[:, 1:2], top[:, 0:1], top_parts[:, GUARD:GUARD + 1],
                                                     ALU.subtract))
                            step.wait()
                            step.inc(V.tensor_copy(top_parts[:, GUARD + 1:GUARD + 2], top[:, 1:2]))
                            step.wait()
                            V.tensor_tensor(top_parts[:, GUARD + 2:GUARD + 3], top[:, 1:2],
                                            top_parts[:, GUARD + 1:GUARD + 2], ALU.subtract)\
                             .then_inc(row_parts, 1)
                            dve.wait_ge(row_scores, 2 * k + 2)
                            V.tensor_copy(qh[g % 2][GUARD:P, hh, bass.ds(t * P, P)],
                                          m_ps[GUARD:P, 0, :].bitcast(BF16)[:, 0:P]).then_inc(row_read, 1)
                with dve.Else():
                    dve.sem_inc(row_step, 4 * GH * NT)
                    dve.sem_inc(row_parts, GH * NT)
                    dve.sem_inc(row_read, 2 * GH * NT)

            def slot(b, s, kind):
                g = s // NT
                if s % NT == 0:
                    if s == 0:
                        dve.wait_ge(fold_ready, b + 1)
                        pass_wait(dve, passed_dve)
                        dve_wide["now"] = dve.value_load(wide[0:1, 0:1], min_val=0, max_val=1)
                        row_maxima(b, 0)
                    if g + 1 < NG:
                        set_guard(b, g + 1)
                        row_maxima(b, g + 1)
                elif s % NT == 2:
                    if s > 2:
                        invert(b, g - 1)
                    elif not starts(b, 0):
                        invert(b - 1, NG - 1)

            def close():
                invert(B - 1, NG - 1)

            run(setup, items_of, slot, close, dve)


_INS = ["x", "L0_tok_projection", "L0_attn_W_qkv", "L0_attn_b_qkv", "L0_attn_W_proj",
        "L0_attn_b_proj", "L0_ffn_W1", "L0_ffn_b1", "L0_ffn_W2", "L0_ffn_b2"]


def kernel(**inputs):
    import numpy as np
    import concourse.bacc as bacc
    from concourse.bass_utils import run_bass_kernel_spmd

    nc = bacc.Bacc("TRN2", target_bir_lowering=False, num_devices=1)
    arrays, args = {}, []
    for name in _INS:
        a = np.ascontiguousarray(inputs[name])
        arrays[f"in_{name}"] = a
        args.append(nc.dram_tensor(f"in_{name}", a.shape, mybir.dt.from_np(a.dtype), kind="ExternalInput").ap())
    out = nc.dram_tensor("out_h", (B, N, D), F32, kind="ExternalOutput").ap()
    block_kernel(nc, *args, out)
    r = run_bass_kernel_spmd(nc, [arrays], core_ids=[0])
    return r.results[0]["out_h"]
```
